# Optimizing a Trainium2 kernel written in Bass

```python
import numpy as np
import jax
import jax.numpy as jnp

def _softmax(x, axis=-1):
    return jax.nn.softmax(x, axis=axis)

def _gelu(x):
    return jax.nn.gelu(x, approximate=True)

def _silu(x):
    return jax.nn.silu(x)

def _sigmoid(x):
    return jax.nn.sigmoid(x)

def _layernorm(x, axis=-1, eps=1e-05):
    m = jnp.mean(x, axis=axis, keepdims=True)
    v = jnp.var(x, axis=axis, keepdims=True)
    return (x - m) / jnp.sqrt(v + eps)

def _scatter_add(tgt, idx, src, axis=0):
    return tgt.at[idx].add(src)

def _segment_sum(src, seg, n):
    return jax.ops.segment_sum(src, seg, n)
kernel_name = 'mk_hybrid_d1_jaxref_r4_00306e'

def setup_inputs(seed: int=0):
    np.random.seed(seed)
    _w = jnp.asarray

    def _L0_attn_a_setup():
        import jax, jax.numpy as jnp
        import numpy as np
        import math
        DIM = 256
        HEADS = 16
        HEAD_DIM = DIM // HEADS
        key = jax.random.key(seed)
        ks = jax.random.split(key, 7)
        b, n = (2, 512)
        scale = 1.0 / math.sqrt(DIM)
        x = jax.random.normal(ks[0], (b, n, DIM), dtype=jnp.float32)
        Wq = jax.random.normal(ks[1], (DIM, DIM), dtype=jnp.float32) * scale
        Wk = jax.random.normal(ks[2], (DIM, DIM), dtype=jnp.float32) * scale
        Wv = jax.random.normal(ks[3], (DIM, DIM), dtype=jnp.float32) * scale
        Wo = jax.random.normal(ks[4], (DIM, DIM), dtype=jnp.float32) * scale
        bo = jnp.zeros((DIM,), dtype=jnp.float32)
        denom_bias = jnp.zeros((1, HEADS, 1, 1), dtype=jnp.float32)
        return {'x': x, 'Wq': Wq, 'Wk': Wk, 'Wv': Wv, 'Wo': Wo, 'bo': bo, 'denom_bias': denom_bias}
    _L0_attn_a_in = _L0_attn_a_setup()

    def _L0_attn_b_setup():
        import jax, jax.numpy as jnp
        import numpy as np
        key = jax.random.key(seed)
        ks = jax.random.split(key, 5)
        B, S, D = (2, 512, 256)
        scale = 0.02
        return {'x': jax.random.normal(ks[0], (B, S, D), dtype=jnp.float32), 'q_proj_weight': jax.random.normal(ks[1], (D, D), dtype=jnp.float32) * scale, 'k_proj_weight': jax.random.normal(ks[2], (D, D), dtype=jnp.float32) * scale, 'v_proj_weight': jax.random.normal(ks[3], (D, D), dtype=jnp.float32) * scale, 'o_proj_weight': jax.random.normal(ks[4], (D, D), dtype=jnp.float32) * scale}
    _L0_attn_b_in = _L0_attn_b_setup()

    def _L0_ffn_setup():
        import jax, jax.numpy as jnp
        import numpy as np
        T, Z, D_DIM = (8, 512, 256)
        N_EXP, P_SLOT, H = (64, 32, 256)
        LN_EPS = 1e-05
        key = jax.random.key(seed)
        k = jax.random.split(key, 5)
        s = 0.02
        return {'x': jax.random.normal(k[0], (T, Z, D_DIM), dtype=jnp.float32), 'phi_w': jax.random.normal(k[1], (N_EXP * P_SLOT, D_DIM), dtype=jnp.float32) * s, 'phi_b': jax.random.normal(k[2], (N_EXP * P_SLOT,), dtype=jnp.float32) * s, 'expert_w': jax.random.normal(k[3], (N_EXP, D_DIM, H), dtype=jnp.float32) * s, 'expert_b': jax.random.normal(k[4], (N_EXP, H), dtype=jnp.float32) * s}
    _L0_ffn_in = _L0_ffn_setup()
    _d = {'L0_attn_a_x': _L0_attn_a_in['x'], 'L0_attn_a_Wq': _L0_attn_a_in['Wq'], 'L0_attn_a_Wk': _L0_attn_a_in['Wk'], 'L0_attn_a_Wv': _L0_attn_a_in['Wv'], 'L0_attn_a_Wo': _L0_attn_a_in['Wo'], 'L0_attn_a_bo': _L0_attn_a_in['bo'], 'L0_attn_a_denom_bias': _L0_attn_a_in['denom_bias'], 'L0_attn_b_q_proj_weight': _L0_attn_b_in['q_proj_weight'], 'L0_attn_b_k_proj_weight': _L0_attn_b_in['k_proj_weight'], 'L0_attn_b_v_proj_weight': _L0_attn_b_in['v_proj_weight'], 'L0_attn_b_o_proj_weight': _L0_attn_b_in['o_proj_weight'], 'L0_ffn_phi_w': _L0_ffn_in['phi_w'], 'L0_ffn_phi_b': _L0_ffn_in['phi_b'], 'L0_ffn_expert_w': _L0_ffn_in['expert_w'], 'L0_ffn_expert_b': _L0_ffn_in['expert_b']}
    _x0 = _d['L0_attn_a_x']
    _d['L0_attn_a_x'] = jax.random.normal(jax.random.fold_in(jax.random.key(seed), 1), (1, 4096, 256), dtype=_x0.dtype)
    del _x0
    return _d

def reference(L0_attn_a_x, L0_attn_a_Wq, L0_attn_a_Wk, L0_attn_a_Wv, L0_attn_a_Wo, L0_attn_a_bo, L0_attn_a_denom_bias, L0_attn_b_q_proj_weight, L0_attn_b_k_proj_weight, L0_attn_b_v_proj_weight, L0_attn_b_o_proj_weight, L0_ffn_phi_w, L0_ffn_phi_b, L0_ffn_expert_w, L0_ffn_expert_b):

    def _L0_attn_a_ref(x, Wq, Wk, Wv, Wo, bo, denom_bias):
        import jax, jax.numpy as jnp
        import numpy as np
        import math
        DIM = 256
        HEADS = 16
        HEAD_DIM = DIM // HEADS
        b, n, d = x.shape
        h, hd = (HEADS, HEAD_DIM)

        def split_heads(t):
            return t.reshape(b, n, h, hd).transpose(0, 2, 1, 3)
        q = split_heads(x @ Wq.T)
        k = split_heads(x @ Wk.T)
        v = split_heads(x @ Wv.T)
        sim = jnp.einsum('bhid,bhjd->bhij', q, k) / math.sqrt(hd)
        causal_mask = jnp.triu(jnp.ones((n, n), dtype=bool), k=1)
        neg = -jnp.finfo(sim.dtype).max
        sim = jnp.where(causal_mask, neg, sim)
        sim_max = jnp.max(sim, axis=-1, keepdims=True)
        exp_sim = jnp.exp(sim - sim_max)
        denom = jnp.sum(exp_sim, axis=-1, keepdims=True) + jnp.exp(denom_bias)
        attn = exp_sim / denom
        out = jnp.einsum('bhij,bhjd->bhid', attn, v)
        out = out.transpose(0, 2, 1, 3).reshape(b, n, d)
        return out @ Wo.T + bo

    def _L0_attn_b_ref(x, q_proj_weight, k_proj_weight, v_proj_weight, o_proj_weight):
        import jax, jax.numpy as jnp
        import numpy as np
        num_heads = 16
        B, S, d_in = x.shape
        d_k = q_proj_weight.shape[0]
        head_size = d_k // num_heads

        def split_heads(t):
            return t.reshape(B, S, num_heads, head_size).transpose(0, 2, 1, 3)
        q = split_heads(jnp.einsum('bsd,kd->bsk', x, q_proj_weight))
        k = split_heads(jnp.einsum('bsd,kd->bsk', x, k_proj_weight))
        v = split_heads(jnp.einsum('bsd,kd->bsk', x, v_proj_weight))
        scale = jnp.float32(head_size) ** (-0.5)
        scores = jnp.einsum('bhtc,bhkc->bhtk', q, k) * scale
        causal = jnp.tril(jnp.ones((S, S), dtype=bool))
        scores = jnp.where(causal, scores, -jnp.inf)
        attn = jax.nn.softmax(scores, axis=-1)
        out = jnp.einsum('bhtk,bhkc->bhtc', attn, v)
        out = out.transpose(0, 2, 1, 3).reshape(B, S, d_k)
        return jnp.einsum('bsv,dv->bsd', out, o_proj_weight)

    def _L0_ffn_ref(x, phi_w, phi_b, expert_w, expert_b):
        import jax, jax.numpy as jnp
        import numpy as np
        T, Z, D_DIM = (8, 512, 256)
        N_EXP, P_SLOT, H = (64, 32, 256)
        LN_EPS = 1e-05
        t, z, d = x.shape
        n = expert_w.shape[0]
        p = phi_w.shape[0] // n
        logits = (jnp.einsum('tzd,ed->tze', x, phi_w) + phi_b).reshape(t, z, n, p)
        D = jax.nn.softmax(logits, axis=3)
        C = jax.nn.softmax(logits, axis=2)
        X_tilde = jnp.einsum('tznp,tzd->npd', D, x)
        X_tilde = jnp.clip(X_tilde, -33000.0, 65000.0)
        mu = jnp.mean(X_tilde, axis=-1, keepdims=True)
        var = jnp.mean(jnp.square(X_tilde - mu), axis=-1, keepdims=True)
        X_tilde = (X_tilde - mu) * jax.lax.rsqrt(var + LN_EPS)
        X_tilde = jnp.tanh(X_tilde)
        Y_tilde = jnp.einsum('npd,ndH->npH', X_tilde, expert_w) + expert_b[:, None, :]
        Y = jnp.einsum('tznp,npH->tzH', C, Y_tilde)
        return Y
    x = L0_attn_a_x
    x = x + _L0_attn_a_ref(_layernorm(x, axis=-1), L0_attn_a_Wq, L0_attn_a_Wk, L0_attn_a_Wv, L0_attn_a_Wo, L0_attn_a_bo, L0_attn_a_denom_bias)
    x = x + _L0_ffn_ref(_layernorm(x, axis=-1), L0_ffn_phi_w, L0_ffn_phi_b, L0_ffn_expert_w, L0_ffn_expert_b)
    x = x + _L0_attn_b_ref(_layernorm(x, axis=-1), L0_attn_b_q_proj_weight, L0_attn_b_k_proj_weight, L0_attn_b_v_proj_weight, L0_attn_b_o_proj_weight)
    x = x + _L0_ffn_ref(_layernorm(x, axis=-1), L0_ffn_phi_w, L0_ffn_phi_b, L0_ffn_expert_w, L0_ffn_expert_b)
    return x

_drawn_inputs = setup_inputs


def setup_inputs(seed=0):
    import zlib

    import numpy as np

    out = dict(_drawn_inputs(seed))
    spreads = {'L0_attn_a_bo': (0.0, 0.1), 'L0_attn_a_denom_bias': (0.0, 2.0)}
    factors = {'L0_attn_b_q_proj_weight': 8.0, 'L0_attn_b_k_proj_weight': 8.0, 'L0_ffn_phi_b': 8.0}
    for name, (base, spread) in spreads.items():
        noise = np.random.default_rng([zlib.crc32(name.encode()), seed]).standard_normal(out[name].shape)
        drawn = base * np.exp(spread * noise) if base else spread * noise
        out[name] = jnp.asarray(drawn.astype(out[name].dtype))
    for name, factor in factors.items():
        out[name] = (out[name] * factor).astype(out[name].dtype)
    return out
```

```python
from contextlib import ExitStack, contextmanager

import concourse.bass as bass
from concourse import mybir

F32 = mybir.dt.float32
BF16 = mybir.dt.bfloat16
ALU = mybir.AluOpType
ACT = mybir.ActivationFunctionType
AX = mybir.AxisListType

P = 128
N, D = 4096, 256
T = N // P
DC = D // P
HEADS, HD = 16, 16
SCALE = float(HD) ** -0.5
EPS = 1e-5
NEG = -3.0e38
BANK = 512
TERMS_Q = (0, 1, 0, 1, 2, 0)
TERMS_K = (0, 0, 1, 1, 0, 2)
ROWS = HD * len(TERMS_Q)
ROWS_M = ROWS + 3
VW = 32
G = N // BANK
KB = BANK // P
SLOTS, NE, PS = 2048, 64, 32
EB = SLOTS // P


class Kept:
    pass


@contextmanager
def phase_of(nc, tag):
    sems = []

    def sem(name):
        sems.append(nc.alloc_semaphore(f"{tag}_{name}"))
        return sems[-1]

    with ExitStack() as ctx:
        yield ctx, sem, lambda name, shape, dt=F32: ctx.enter_context(nc.sbuf_tensor(f"{tag}_{name}", shape, dt))
    nc.clear_and_free_semaphores(sems)
    nc.all_engine_barrier(sem_only=True)


def wait(eng, sem, value):
    if isinstance(value, int) and value <= 0:
        return
    eng.wait_ge(sem, value)


def load_and_constants(nc, m, x_in):
    with phase_of(nc, "consts") as (ctx, sem, sb):
        x_loaded, cleared, built = sem("x_loaded"), sem("cleared"), sem("built")
        block = ctx.enter_context(nc.Block())

        @block.sync
        def _(sp):
            sp.dma_start(m.x[:, :, :], x_in.rearrange("a (t p) d -> p (a t) d", p=P)).then_inc(x_loaded, 16)
            sp.wait_ge(x_loaded, 16)

        @block.vector
        def _(dve):
            for t in (m.ident, m.identb, m.mask_qk, m.sel, m.same, m.sameneg):
                dve.memset(t[:, :], 0.0)
            dve.memset(m.onesb[:, :], 1.0).then_inc(cleared, 1)

        @block.gpsimd
        def _(pool):
            pool.wait_ge(cleared, 1)
            for t in (m.ident, m.identb):
                pool.affine_select(out=t[:, :], in_=t[:, :], pattern=[[-1, P]], compare_op=ALU.not_equal,
                                   fill=1.0, base=0, channel_multiplier=1)
            pool.affine_select(out=m.mask_qk[:, :], in_=m.mask_qk[:, :], pattern=[[-1, P]],
                               compare_op=ALU.is_ge, fill=NEG, base=0, channel_multiplier=1).then_inc(built, 1)
            n = 1
            for j in range(4):
                for t, pattern, fill in ((m.sel[:, :], [[-1, HD + 1]], 1.0),
                                         (m.same[:, :].rearrange("p (a c) -> p a c", a=4), [[0, 4], [-1, 32]], 1.0),
                                         (m.sameneg[:, :].rearrange("p (a c) -> p a c", a=4), [[0, 4], [-1, 32]], -1.0)):
                    pool.wait_ge(built, n)
                    pool.affine_select(out=t, in_=t, pattern=pattern, compare_op=ALU.not_equal,
                                       fill=fill, base=-32 * j, channel_multiplier=1).then_inc(built, 1)
                    n += 1
            pool.wait_ge(built, n)


def transposed(nc, ps, tag, src, dst, after=None):
    jobs = [(tg, c) for tg in range(T // 4) for c in range(DC)]

    def pe_part(pe, ident, ready, filled, act_copied, dve_copied):
        for i, (tg, c) in enumerate(jobs):
            ready(pe, 4 * tg + 4)
            if i >= 4:
                wait(pe, act_copied if i % 2 == 0 else dve_copied, (i - 4) // 2 + 1)
            for k in range(4):
                mm = pe.transpose(ps[:, (i % 4) * BANK + k * P:(i % 4) * BANK + (k + 1) * P],
                                  src[:, 4 * tg + k, c * P:(c + 1) * P], ident)
            mm.then_inc(filled, 1)

    def copy_part(eng, copy, odd, filled, copied):
        for i, (tg, c) in enumerate(jobs):
            if i % 2 == odd:
                eng.wait_ge(filled, i + 1)
                copy(dst[:, c, tg * BANK:(tg + 1) * BANK], ps[:, (i % 4) * BANK:(i % 4 + 1) * BANK]).then_inc(copied, 1)

    return pe_part, copy_part


def layernorm(nc, m, ps, tag, xln, xlnT):
    with phase_of(nc, tag) as (ctx, sem, sb):
        stats, mv = sb("stats", [P, T, 6]), sb("mv", [P, T, 2])
        ve, sd, rs = sb("ve", [P, T]), sb("sd", [P, T]), sb("rs", [P, T])
        stats_done, mv_done, ve_done, sd_done = sem("stats_done"), sem("mv_done"), sem("ve_done"), sem("sd_done")
        rs_done, normed = sem("rs_done"), sem("normed")
        filled, act_copied, dve_copied = sem("filled"), sem("act_copied"), sem("dve_copied")
        pe_part, copy_part = transposed(nc, ps, tag, xln, xlnT)
        block = ctx.enter_context(nc.Block())

        @block.vector
        def _(dve):
            for t in range(T):
                dve.bn_stats(stats[:, t, :], m.x[:, t, :]).then_inc(stats_done, 1)
            for t in range(T):
                dve.wait_ge(stats_done, t + 1)
                dve.bn_aggr(mv[:, t, :], stats[:, t, :]).then_inc(mv_done, 1)
            dve.wait_ge(mv_done, T)
            dve.tensor_scalar(ve[:, :], mv[:, :, 1], EPS, None, ALU.add).then_inc(ve_done, 1)
            dve.wait_ge(sd_done, 1)
            dve.reciprocal(rs[:, :], sd[:, :]).then_inc(rs_done, 1)
            dve.wait_ge(rs_done, 1)
            for t in range(T):
                dve.tensor_scalar(xln[:, t, :], m.x[:, t, :], mv[:, t, 0:1], rs[:, t:t + 1],
                                  ALU.subtract, ALU.mult).then_inc(normed, 1)
            copy_part(dve, dve.tensor_copy, 1, filled, dve_copied)

        @block.scalar
        def _(act):
            act.wait_ge(ve_done, 1)
            act.activation(sd[:, :], ve[:, :], ACT.Sqrt).then_inc(sd_done, 1)
            copy_part(act, act.copy, 0, filled, act_copied)

        @block.tensor
        def _(pe):
            pe_part(pe, m.ident[:, :], lambda eng, n: eng.wait_ge(normed, n), filled, act_copied, dve_copied)


def project_qkv(nc, m, ps, tag, xlnT, v, wq, wk, wv, parts_q, parts_k):
    HALF = N // 2
    NB = HALF // BANK
    with phase_of(nc, tag) as (ctx, sem, sb):
        w = [sb(f"w{i}", [P, DC, D]) for i in range(3)]
        cut = sb("cut", [P, 2, 3, HALF], BF16)
        rest = sb("rest", [P, 2, BANK])
        w_loaded = [sem(f"w_loaded{i}") for i in range(3)]
        made = sem("made")
        high = sem("high")
        left = sem("left")
        mid = sem("mid")
        low = sem("low")
        stored = [sem("stored0"), sem("stored1")]
        v_made, v_kept = sem("v_made"), sem("v_kept")
        block = ctx.enter_context(nc.Block())
        jobs = [(i, oc, hf) for oc in range(DC) for i in range(2) for hf in range(2)]

        @block.sync
        def _(sp):
            for i, wi in enumerate((wq, wk, wv)):
                sp.dma_start(w[i][:, :, :], wi.rearrange("(c p) o -> p c o", p=P)).then_inc(w_loaded[i], 16)
            for j, (i, oc, hf) in enumerate(jobs):
                sp.wait_ge(low, NB * (j + 1))
                dst = (parts_q, parts_k)[i]
                for part in range(3):
                    sp.dma_start(dst[part, oc * P:(oc + 1) * P, hf * HALF:(hf + 1) * HALF],
                                 cut[:, j % 2, part, :]).then_inc(stored[j % 2], 16)
            for s in stored:
                sp.wait_ge(s, 48 * len(jobs) // 2)

        @block.tensor
        def _(pe):
            n = 0
            for j, (i, oc, hf) in enumerate(jobs):
                if oc == 0 and hf == 0:
                    pe.wait_ge(w_loaded[i], 16)
                for b in range(NB):
                    wait(pe, left, n - 3)
                    for c in range(DC):
                        mm = pe.matmul(ps[:, (n % 4) * BANK:(n % 4 + 1) * BANK], w[i][:, c, oc * P:(oc + 1) * P],
                                       xlnT[:, c, hf * HALF + b * BANK:hf * HALF + (b + 1) * BANK],
                                       start=(c == 0), stop=(c == DC - 1))
                    mm.then_inc(made, 1)
                    n += 1
            pe.wait_ge(w_loaded[2], 16)
            for t in range(T):
                wait(pe, v_kept, t - 3)
                for c in range(DC):
                    mm = pe.matmul(ps[:, (4 + t % 4) * BANK:(4 + t % 4) * BANK + D], xlnT[:, c, t * P:(t + 1) * P],
                                   w[2][:, c, :], start=(c == 0), stop=(c == DC - 1))
                mm.then_inc(v_made, 1)

        @block.scalar
        def _(act):
            n = 0
            for j, (i, oc, hf) in enumerate(jobs):
                scale = SCALE if i == 0 else 1.0
                wait(act, stored[j % 2], 48 * (j // 2))
                for b in range(NB):
                    act.wait_ge(made, n + 1)
                    act.activation(cut[:, j % 2, 0, b * BANK:(b + 1) * BANK], ps[:, (n % 4) * BANK:(n % 4 + 1) * BANK],
                                   ACT.Copy, scale=scale).then_inc(high, 1)
                    act.wait_ge(left, n + 1)
                    act.activation(cut[:, j % 2, 1, b * BANK:(b + 1) * BANK], rest[:, n % 2, :],
                                   ACT.Copy).then_inc(mid, 1)
                    n += 1
            for t in range(T):
                act.wait_ge(v_made, t + 1)
                act.activation(v[:, t, :], ps[:, (4 + t % 4) * BANK:(4 + t % 4) * BANK + D], ACT.Copy).then_inc(v_kept, 1)

        @block.vector
        def _(dve):
            n = 0
            for j, (i, oc, hf) in enumerate(jobs):
                scale = SCALE if i == 0 else 1.0
                for b in range(NB):
                    dve.wait_ge(high, n + 1)
                    wait(dve, low, n - 1)
                    dve.scalar_tensor_tensor(rest[:, n % 2, :], ps[:, (n % 4) * BANK:(n % 4 + 1) * BANK], scale,
                                             cut[:, j % 2, 0, b * BANK:(b + 1) * BANK],
                                             ALU.mult, ALU.subtract).then_inc(left, 1)
                    dve.wait_ge(left, n + 1)
                    dve.wait_ge(mid, n + 1)
                    dve.tensor_tensor(cut[:, j % 2, 2, b * BANK:(b + 1) * BANK], rest[:, n % 2, :],
                                      cut[:, j % 2, 1, b * BANK:(b + 1) * BANK], ALU.subtract).then_inc(low, 1)
                    n += 1


def chunks():
    out = []
    for t in range(T):
        last = t // 4
        for c in range(last + 1):
            out.append((t, c, BANK if c < last else P * (t % 4 + 1), c == last))
    return out


HALF_T = T // 2
CUTS = 5
CHUNKS = chunks()
CHUNKS_A = sum(t < HALF_T for t, _, _, _ in CHUNKS)
FIRST_ITEMS = CHUNKS[:CHUNKS_A + 4] + ["A"] + CHUNKS[CHUNKS_A + 4:]
ITEMS = FIRST_ITEMS[:4] + ["B"] + FIRST_ITEMS[4:]
N_FIRST, N_ITEMS = len(FIRST_ITEMS), len(ITEMS)
STEPS = [(g, c) for g in range(G) for c in range(g + 1)]
TAIL_ITEMS = 8
ITEMS_BY = [(N_ITEMS - TAIL_ITEMS) * (s + 1) // len(STEPS) for s in range(len(STEPS))]
RING = 3


def attention(nc, m, ps, tag, v, attn, parts_q, parts_k, denom_bias):
    NS = len(STEPS)
    with phase_of(nc, tag) as (ctx, sem, sb):
        q1 = [sb(f"q1_{i}", [P, N], BF16) for i in range(2)]
        k1 = [sb(f"k1_{i}", [P, N], BF16) for i in range(2)]
        q2 = [sb(f"q2_{i}", [P, N], BF16) for i in range(2)]
        k2 = [sb(f"k2_{i}", [P, N], BF16) for i in range(2)]
        vh = [sb(f"vh_{i}", [P, T, VW]) for i in range(2)]
        pt = sb("pt", [P, 2 * KB, BANK])
        osb = sb("osb", [P, 2, BANK])
        mx = sb("mx", [P, T, G])
        mfull = sb("mfull", [P, HALF_T])
        mrest = sb("mrest", [P, HALF_T])
        m3all = sb("m3", [P, P], BF16)
        m3 = m3all[:, 0:3 * HALF_T].rearrange("p (a t) -> p a t", a=3)
        mt = [sb(f"mt_{i}", [3 * HALF_T, P], BF16) for i in range(2)]
        den = sb("den", [P, HALF_T])
        rden = sb("rden", [P, HALF_T])
        dbias = sb("dbias", [P, HEADS])

        SCORES_T, SCORES = 0, RING
        OUT = ps[:, 6 * BANK:7 * BANK]
        TURNED = ps[:, 7 * BANK:7 * BANK + HALF_T * (HD + 1)].rearrange("p (t c) -> p t c", c=HD + 1)

        set_up = sem("set_up")
        db_loaded, db_ready = sem("db_loaded"), sem("db_ready")
        p1_loaded = [sem("p1_loaded0"), sem("p1_loaded1")]
        p2_loaded = [sem("p2_loaded0"), sem("p2_loaded1")]
        v_ready = sem("v_ready")
        s1_ready, s1_read = sem("s1_ready"), sem("s1_read")
        m_chain = sem("m_chain")
        mt_ready = sem("mt_ready")
        m_placed = [sem("m_placedA"), sem("m_placedB")]
        st_ready = sem("st_ready")
        pt_ready = sem("pt_ready")
        turns = sem("turns")
        masked = sem("masked")
        pv_done = sem("pv_done")
        o_copied = sem("o_copied")
        turned = sem("turned")
        t_read = sem("t_read")
        d_chain = sem("d_chain")
        block = ctx.enter_context(nc.Block())

        LOADS = 16 * 2 * len(TERMS_Q)

        def first_item(h):
            return N_FIRST + N_ITEMS * h

        def bank_of(n, first):
            return (SCORES + (n + N_ITEMS - N_FIRST if first else n) % RING) * BANK

        def phases(eng, phase):
            with eng.Fori(0, HEADS // 2 - 1) as it:
                for parity in range(2):
                    phase(it, parity, True)
            phase(HEADS // 2 - 1, 0, True)
            phase(HEADS // 2 - 1, 1, False)

        @block.sync
        def _(sp):
            def load(q, k, h, loaded):
                for dst, src, terms in ((q, parts_q, TERMS_Q), (k, parts_k, TERMS_K)):
                    for r, part in enumerate(terms):
                        sp.dma_start(dst[r * HD:(r + 1) * HD, :], src[part, bass.ds(h * HD, HD), :]).then_inc(loaded, 16)

            def place(half, parity):
                for part in range(3):
                    sp.dma_start(q2[parity][ROWS + part:ROWS + part + 1, half * N // 2:(half + 1) * N // 2],
                                 mt[half][part * HALF_T:(part + 1) * HALF_T, :]).then_inc(m_placed[half], 16)

            if denom_bias is not None:
                sp.dma_start(dbias[:, :], denom_bias.rearrange("a h b c -> (a b c) h").partition_broadcast(P)
                             ).then_inc(db_loaded, 16)
            load(q1[0], k1[0], 0, p1_loaded[0])
            load(q2[0], k2[0], 0, p2_loaded[0])
            load(q1[1], k1[1], 1, p1_loaded[1])
            sp.wait_ge(mt_ready, 1)
            sp.wait_ge(set_up, 1)
            place(0, 0)

            def phase(it, parity, more):
                h = 2 * it + parity
                if more:
                    sp.wait_ge(st_ready, KB * NS * h + 1)
                    load(q2[1 - parity], k2[1 - parity], h + 1, p2_loaded[1 - parity])
                    if not (isinstance(h, int) and h == HEADS - 2):
                        sp.wait_ge(s1_ready, first_item(h))
                        load(q1[parity], k1[parity], h + 2, p1_loaded[parity])
                sp.wait_ge(mt_ready, 2 * h + 2)
                place(1, parity)
                if more:
                    sp.wait_ge(mt_ready, 2 * h + 3)
                    place(0, 1 - parity)
            phases(sp, phase)
            for s in m_placed:
                sp.wait_ge(s, 48 * HEADS)

        @block.gpsimd
        def _(pool):
            for s, n in ((st_ready, 1), (pt_ready, RING), (pv_done, 2), (o_copied, 1), (turned, 2), (t_read, 1)):
                pool.sem_inc(s, n)
            pool.wait_ge(set_up, 1)
            pool.tensor_copy(vh[0][:, :, 0:HD], v[:, :, 0:HD]).then_inc(v_ready, 1)

            def phase(it, parity, more):
                h = 2 * it + parity
                if more:
                    pool.wait_ge(pv_done, NS * h + 2)
                    pool.tensor_copy(vh[1 - parity][:, :, 0:HD], v[:, :, bass.ds((h + 1) * HD, HD)]).then_inc(v_ready, 1)
                for g in range(G):
                    s = STEPS.index((g, g))
                    for j in range(KB):
                        pool.wait_ge(pt_ready, KB * (NS * h + s) + j + 1 + RING)
                        pool.sem_inc(turns, 1)
                        block_p = pt[:, KB * (s % 2) + j, 0:P]
                        pool.affine_select(out=block_p, in_=block_p, pattern=[[1, P]], compare_op=ALU.is_ge,
                                           fill=0.0, base=0, channel_multiplier=-1).then_inc(masked, 1)
            phases(pool, phase)

        @block.tensor
        def _(pe):
            def item(what, i, lag, bank, q, k, chain):
                wait(pe, s1_read, i - lag + 1)
                if what in ("A", "B"):
                    pe.wait_ge(m_chain, chain)
                    pe.transpose(ps[:, bank:bank + P // 2].bitcast(BF16), m3all[:, :], m.identb[:, :]).then_inc(s1_ready, 1)
                    return
                t, c, width, diag = what
                mm = pe.matmul(ps[:, bank:bank + width], q[0:ROWS, t * P:(t + 1) * P],
                               k[0:ROWS, c * BANK:c * BANK + width], start=True, stop=not diag)
                if diag:
                    mm = pe.matmul(ps[:, bank + width - P:bank + width], m.identb[:, :], m.mask_qk[:, :],
                                   start=False, stop=True)
                mm.then_inc(s1_ready, 1)

            pe.wait_ge(p1_loaded[0], LOADS)
            for i, what in enumerate(FIRST_ITEMS):
                item(what, i, RING, bank_of(i, True), q1[0], k1[0], CUTS)
            pe.wait_ge(set_up, 1)

            def phase(it, parity, more):
                h = 2 * it + parity
                q, k = q2[parity], k2[parity]
                items = ITEMS if more else ["B"]
                done = [0]

                def run_items(upto):
                    for n in range(done[0], min(upto, len(items))):
                        item(items[n], first_item(h) + n, 2 if n < 2 else RING, bank_of(n, False), q1[1 - parity], k1[1 - parity],
                             2 * CUTS * h + (3 * CUTS if items[n] == "A" else 2 * CUTS))
                        done[0] = n + 1

                def scores_t(s, j):
                    g, c = STEPS[s]
                    kb, width = KB * c + j, BANK - P * j if c == g else BANK
                    bank = (SCORES_T + (KB * s + j) % RING) * BANK
                    pe.wait_ge(pt_ready, KB * (NS * h + s) + j + 1)
                    pe.matmul(ps[:, bank:bank + width], k[0:ROWS_M, kb * P:(kb + 1) * P],
                              q[0:ROWS_M, (g + 1) * BANK - width:(g + 1) * BANK],
                              start=True, stop=True).then_inc(st_ready, 1)

                def p_v(s):
                    g, c = STEPS[s]
                    if c == g:
                        pe.wait_ge(masked, KB * (G * h + g) + KB)
                    else:
                        pe.wait_ge(pt_ready, KB * (NS * h + s) + KB + RING)
                    if c == 0:
                        pe.wait_ge(o_copied, G * h + g + 1)
                    for j in range(KB):
                        width = BANK - P * j if c == g else BANK
                        mm = pe.matmul(OUT[32 * j:32 * j + VW, BANK - width:BANK], vh[parity][:, KB * c + j, :],
                                       pt[:, KB * (s % 2) + j, 0:width], start=(c == 0), stop=(c == g))
                    mm.then_inc(pv_done, 1)

                def turn(g):
                    pe.wait_ge(o_copied, G * h + g + 2)
                    if g % 4 == 0:
                        pe.wait_ge(t_read, 2 * h + g // 4 + 1)
                    for k4 in range(4):
                        rows = P if g else 32 * (k4 + 1)
                        mm = pe.matmul(TURNED[:, 4 * (g % 4) + k4, :], osb[0:rows, g % 2, k4 * P:(k4 + 1) * P],
                                       m.sel[0:rows, :], start=True, stop=True)
                    mm.then_inc(turned, 1)

                pe.wait_ge(p2_loaded[parity], LOADS * (it + 1))
                pe.wait_ge(m_placed[0], 48 * (h + 1))
                pe.wait_ge(v_ready, h + 1)
                if more:
                    pe.wait_ge(p1_loaded[1 - parity], LOADS * (it + 1 + parity))
                for s, (g, c) in enumerate(STEPS):
                    if g == G // 2 and c == 0:
                        pe.wait_ge(m_placed[1], 48 * (h + 1))
                    before = ITEMS_BY[s - 1] if s else 0
                    for j in range(KB):
                        scores_t(s, j)
                        run_items(before + (ITEMS_BY[s] - before) * (j + 1) // KB)
                    if s >= 2 and STEPS[s - 2][0] == STEPS[s - 2][1]:
                        turn(STEPS[s - 2][0])
                    if s:
                        p_v(s - 1)
                run_items(N_ITEMS - TAIL_ITEMS // 2)
                p_v(NS - 1)
                run_items(N_ITEMS)
                turn(G - 1)
            phases(pe, phase)

        @block.scalar
        def _(act):
            if denom_bias is not None:
                act.wait_ge(db_loaded, 16)
                act.activation(dbias[:, :], dbias[:, :], ACT.Exp).then_inc(db_ready, 1)

            def phase(it, parity, more):
                h = 2 * it + parity

                def copy_group(g):
                    act.wait_ge(pv_done, NS * h + (g + 1) * (g + 2) // 2 + 2)
                    act.wait_ge(turned, G * h + g + 1)
                    if g:
                        last = act.activation(osb[:, g % 2, :], OUT, ACT.Copy)
                    else:
                        for j in range(KB):
                            last = act.activation(osb[32 * j:32 * j + VW, 0, P * j:BANK],
                                                  OUT[32 * j:32 * j + VW, P * j:BANK], ACT.Copy)
                    last.then_inc(o_copied, 1)

                for s, (g, c) in enumerate(STEPS):
                    act.wait_ge(pv_done, NS * h + s + 1)
                    for j in range(KB):
                        bank = (SCORES_T + (KB * s + j) % RING) * BANK
                        width = BANK - P * j if c == g else BANK
                        act.wait_ge(st_ready, KB * (NS * h + s) + j + 2)
                        act.activation(pt[:, KB * (s % 2) + j, 0:width], ps[:, bank:bank + width], ACT.Exp).then_inc(pt_ready, 1)
                        if j == 1 and s >= 2 and STEPS[s - 2][0] == STEPS[s - 2][1]:
                            copy_group(STEPS[s - 2][0])
                copy_group(G - 1)
            phases(act, phase)

        @block.vector
        def _(dve):
            dve.memset(mx[:, :, :], NEG)
            for i in range(2):
                dve.memset(k2[i][ROWS:ROWS_M, :], -1.0)
                dve.memset(vh[i][:, :, HD + 1:VW], 0.0)
                dve.memset(vh[i][:, :, HD:HD + 1], 1.0)
            dve.memset(m3all[:, :], 0.0).then_inc(set_up, 1)
            dve.wait_ge(set_up, 1)

            def item(what, i, bank):
                dve.wait_ge(s1_ready, i + 1)
                if what in ("A", "B"):
                    half = "AB".index(what)
                    dve.tensor_copy(mt[half][:, :], ps[0:3 * HALF_T, bank:bank + P // 2].bitcast(BF16)).then_inc(s1_read, 1)
                    dve.wait_ge(s1_read, i + 1)
                    dve.sem_inc(mt_ready, 1)
                    return
                t, c, width, _ = what
                dve.tensor_reduce(mx[:, t, c:c + 1], ps[:, bank:bank + width], AX.X, ALU.max).then_inc(s1_read, 1)

            def cut_maxima(half, i, base):
                dve.wait_ge(s1_read, i + 1)
                dve.tensor_reduce(mfull[:, :], mx[:, half * HALF_T:(half + 1) * HALF_T, 0:(half + 1) * G // 2],
                                  AX.X, ALU.max).then_inc(m_chain, 1)
                dve.wait_ge(m_chain, base + 1)
                dve.tensor_copy(m3[:, 0, :], mfull[:, :]).then_inc(m_chain, 1)
                dve.wait_ge(m_chain, base + 2)
                dve.tensor_tensor(mrest[:, :], mfull[:, :], m3[:, 0, :], ALU.subtract).then_inc(m_chain, 1)
                dve.wait_ge(m_chain, base + 3)
                dve.tensor_copy(m3[:, 1, :], mrest[:, :]).then_inc(m_chain, 1)
                dve.wait_ge(m_chain, base + 4)
                dve.tensor_tensor(m3[:, 2, :], mrest[:, :], m3[:, 1, :], ALU.subtract).then_inc(m_chain, 1)

            for i, what in enumerate(FIRST_ITEMS):
                item(what, i, bank_of(i, True))
                if i == CHUNKS_A - 1:
                    cut_maxima(0, i, 0)
            cut_maxima(1, N_FIRST - 1, CUTS)
            if denom_bias is not None:
                dve.wait_ge(db_ready, 1)

            def phase(it, parity, more):
                h = 2 * it + parity
                items = ITEMS if more else ["B"]
                done = [0]

                def run_items(upto):
                    for n in range(done[0], min(upto, len(items))):
                        item(items[n], first_item(h) + n, bank_of(n, False))
                        if n == CHUNKS_A:
                            cut_maxima(0, first_item(h) + n, 2 * CUTS * h + 2 * CUTS)
                        done[0] = n + 1

                def divide(half):
                    ops = 1 if denom_bias is None else 2
                    base = ops * (2 * h + half)
                    dve.wait_ge(turned, G * h + 4 * half + 4 + 2)
                    source = TURNED[:, :, HD]
                    if denom_bias is not None:
                        dve.tensor_scalar(den[:, :], source, dbias[:, bass.ds(h, 1)], None, ALU.add).then_inc(d_chain, 1)
                        dve.wait_ge(d_chain, base + 1)
                        source = den[:, :]
                    dve.reciprocal(rden[:, :], source).then_inc(d_chain, 1)
                    dve.wait_ge(d_chain, base + ops)
                    dve.tensor_tensor(attn[:, half * HALF_T:(half + 1) * HALF_T, bass.ds(h * HD, HD)],
                                      TURNED[:, :, 0:HD],
                                      rden[:, :].unsqueeze(2).broadcast_to([P, HALF_T, HD]), ALU.mult).then_inc(t_read, 1)

                run_items(ITEMS_BY[12])
                divide(0)
                run_items(N_ITEMS)
                if more:
                    cut_maxima(1, first_item(h) + N_ITEMS - 1, 2 * CUTS * h + 3 * CUTS)
                divide(1)
            phases(dve, phase)


def project_out(nc, m, ps, tag, attn, wo, bias):
    with phase_of(nc, tag) as (ctx, sem, sb):
        attnT = sb("attnT", [P, DC, N])
        w = sb("w", [P, DC, D])
        brow = sb("brow", [P, D])
        w_loaded, b_loaded = sem("w_loaded"), sem("b_loaded")
        filled, act_copied, dve_copied = sem("filled"), sem("act_copied"), sem("dve_copied")
        biased, made, added = sem("biased"), sem("made"), sem("added")
        pe_part, copy_part = transposed(nc, ps, tag, attn, attnT)
        block = ctx.enter_context(nc.Block())

        @block.sync
        def _(sp):
            sp.dma_start(w[:, :, :], wo.rearrange("(c p) o -> p c o", p=P)).then_inc(w_loaded, 16)
            if bias is not None:
                sp.dma_start(brow[:, :], bias.partition_broadcast(P)).then_inc(b_loaded, 16)

        @block.tensor
        def _(pe):
            pe_part(pe, m.ident[:, :], lambda eng, n: None, filled, act_copied, dve_copied)
            pe.wait_ge(w_loaded, 16)
            pe.wait_ge(act_copied, T // 4)
            pe.wait_ge(dve_copied, T // 4)
            for t in range(T):
                wait(pe, added, t - 3)
                for c in range(DC):
                    mm = pe.matmul(ps[:, (4 + t % 4) * BANK:(4 + t % 4) * BANK + D], attnT[:, c, t * P:(t + 1) * P],
                                   w[:, c, :], start=(c == 0), stop=(c == DC - 1))
                mm.then_inc(made, 1)

        @block.scalar
        def _(act):
            copy_part(act, act.copy, 0, filled, act_copied)

        @block.gpsimd
        def _(pool):
            if bias is not None:
                pool.wait_ge(b_loaded, 16)
                for t in range(T):
                    pool.tensor_tensor(m.x[:, t, :], m.x[:, t, :], brow[:, :], ALU.add).then_inc(biased, 1)

        @block.vector
        def _(dve):
            copy_part(dve, dve.tensor_copy, 1, filled, dve_copied)
            for t in range(T):
                if bias is not None:
                    dve.wait_ge(biased, t + 1)
                dve.wait_ge(made, t + 1)
                dve.tensor_tensor(m.x[:, t, :], ps[:, (4 + t % 4) * BANK:(4 + t % 4) * BANK + D], m.x[:, t, :],
                                  ALU.add).then_inc(added, 1)


def dispatch(nc, m, ps, tag, xln, xlnT, phi, pb3, xacc, mct):
    SUPERS = T // 2
    UNIT = SLOTS // 2
    UN = UNIT // PS
    with phase_of(nc, tag) as (ctx, sem, sb):
        xst = sb("xst", [P, 2, DC, P])
        shifted = sb("shifted", [P, 2, UNIT])
        disp = [sb(f"disp{i}", [P, 4, UNIT]) for i in range(2)]
        md = sb("md", [P, 2, UN])
        sd = sb("sd", [P, 2, UN])
        rd = sb("rd", [P, 2, UN])
        mcp = sb("mcp", [P, 2, PS])
        mc = sb("mc", [P, PS])
        mrest = sb("mrest", [P, PS])
        m3 = sb("m3", [P, 3, PS], BF16)
        LOGITS, XACC, TURN = 0, 4, 6

        cleared = sem("cleared")
        staged = sem("staged")
        l_ready = sem("l_ready")
        sub_done = sem("sub_done")
        md_done = sem("md_done")
        e_done = sem("e_done")
        sum_done = sem("sum_done")
        d_ready = sem("d_ready")
        xa_ready = sem("xa_ready")
        xa_read = sem("xa_read")
        c_chain = sem("c_chain")
        c_turned = sem("c_turned")
        c_kept = sem("c_kept")
        block = ctx.enter_context(nc.Block())

        def supers(eng, run):
            run(0, 0, True, False)
            with eng.Fori(0, SUPERS // 2 - 1) as it:
                run(2 * it + 1, 1, True, True)
                run(2 * it + 2, 0, True, True)
            run(SUPERS - 1, 1, True, True)
            run(SUPERS, 0, False, True)

        @block.scalar
        def _(act):
            def stage(tile, slot):
                act.copy(xst[:, slot, :, :], xlnT[:, :, bass.ds(tile * P, P)]).then_inc(staged, 1)
            stage(0, 0)

            def run(s, parity, logits, products):
                if not logits:
                    return
                wait(act, xa_ready, 8 * s - 7)
                for u in range(4):
                    if u % 2 == 0 and not (u == 2 and isinstance(s, int) and s == SUPERS - 1):
                        wait(act, l_ready, 4 * s + u)
                        stage(2 * s + u // 2 + 1, (u // 2 + 1) % 2)
                    act.wait_ge(sub_done, 4 * s + u + 1)
                    act.activation(disp[parity][:, u, :], shifted[:, u % 2, :], ACT.Exp).then_inc(e_done, 1)
            supers(act, run)

        @block.tensor
        def _(pe):
            def run(s, parity, logits, products):
                for u in range(4):
                    if logits:
                        if u % 2 == 0:
                            pe.wait_ge(staged, 2 * s + u // 2 + 1)
                        wait(pe, sub_done, 4 * s + u - 1)
                        for b in range(UNIT // BANK):
                            out = ps[:, (LOGITS + 2 * (u % 2) + b) * BANK:(LOGITS + 2 * (u % 2) + b + 1) * BANK]
                            e0 = (u % 2) * UNIT + b * BANK
                            for c in range(DC):
                                pe.matmul(out, xst[:, u // 2, c, :], phi[:, c, e0:e0 + BANK], start=(c == 0), stop=False)
                            mm = pe.matmul(out, m.onesb[0:3, :], pb3[0:3, e0:e0 + BANK], start=False, stop=True)
                        mm.then_inc(l_ready, 1)
                    if products:
                        if u == 0:
                            pe.wait_ge(d_ready, 4 * s)
                        for pair in range(2):
                            n = 8 * s - 8 + 2 * u + pair
                            pe.wait_ge(xa_read, n + 1)
                            for e in range(2):
                                eb = 4 * u + 2 * pair + e
                                for tile in range(2):
                                    mm = pe.matmul(ps[:, (XACC + pair) * BANK + e * D:(XACC + pair) * BANK + (e + 1) * D],
                                                   disp[1 - parity][:, 2 * tile + eb // 8, (eb % 8) * P:(eb % 8 + 1) * P],
                                                   xln[:, bass.ds(2 * s - 2 + tile, 1), :].rearrange("p a d -> p (a d)"),
                                                   start=(tile == 0), stop=(tile == 1))
                            mm.then_inc(xa_ready, 1)
                    if logits and u % 2 == 1:
                        tile = 2 * s + u // 2
                        pe.wait_ge(c_chain, 5 * tile + 5)
                        wait(pe, c_kept, tile)
                        pe.transpose(ps[0:3 * PS, TURN * BANK:TURN * BANK + P // 2].bitcast(BF16),
                                     m3[:, :, :].rearrange("p a s -> p (a s)"), m.identb[:, :]).then_inc(c_turned, 1)
            supers(pe, run)

        @block.gpsimd
        def _(pool):
            pool.sem_inc(xa_ready, 1)
            pool.sem_inc(xa_read, 2)

            def run(s, parity, logits, products):
                if not logits:
                    return
                for u in range(4):
                    pool.wait_ge(sum_done, 2 * (4 * s + u) + 2)
                    d = disp[parity][:, u, :].rearrange("p (n q) -> p n q", q=PS)
                    pool.tensor_tensor(d, d, rd[:, u % 2, :].unsqueeze(2).broadcast_to([P, UN, PS]),
                                       ALU.mult).then_inc(d_ready, 1)
            supers(pool, run)

        @block.vector
        def _(dve):
            dve.memset(xacc[:, :, :], 0.0).then_inc(cleared, 1)
            dve.wait_ge(cleared, 1)

            def sums(n, u, parity):
                dve.wait_ge(e_done, n + 1)
                dve.tensor_reduce(sd[:, u % 2, :], disp[parity][:, u, :].rearrange("p (n q) -> p n q", q=PS),
                                  AX.X, ALU.add).then_inc(sum_done, 1)
                dve.wait_ge(sum_done, 2 * n + 1)
                wait(dve, d_ready, n - 1)
                dve.reciprocal(rd[:, u % 2, :], sd[:, u % 2, :]).then_inc(sum_done, 1)

            def keep_turned(tile):
                dve.wait_ge(c_turned, tile + 1)
                dve.tensor_copy(mct[0:3 * PS, bass.ds(tile * P, P)],
                                ps[0:3 * PS, TURN * BANK:TURN * BANK + P // 2].bitcast(BF16)).then_inc(c_kept, 1)

            def run(s, parity, logits, products):
                for u in range(4):
                    n = 4 * s + u
                    if logits:
                        at = (LOGITS + 2 * (u % 2)) * BANK
                        l3 = ps[:, at:at + UNIT].rearrange("p (n q) -> p n q", q=PS)
                        dve.wait_ge(l_ready, n + 1)
                        dve.tensor_reduce(md[:, u % 2, :], l3, AX.X, ALU.max).then_inc(md_done, 1)
                        dve.tensor_reduce(mcp[:, u % 2, :], ps[:, at:at + UNIT].rearrange("p (n q) -> p q n", q=PS),
                                          AX.X, ALU.max).then_inc(md_done, 1)
                        dve.wait_ge(md_done, 2 * n + 1)
                        wait(dve, e_done, n - 1)
                        dve.tensor_tensor(shifted[:, u % 2, :].rearrange("p (n q) -> p n q", q=PS), l3,
                                          md[:, u % 2, :].unsqueeze(2).broadcast_to([P, UN, PS]),
                                          ALU.subtract).then_inc(sub_done, 1)
                        if u % 2 == 1:
                            tile = 2 * s + u // 2
                            base = 5 * tile
                            dve.wait_ge(md_done, 2 * n + 2)
                            dve.tensor_tensor(mc[:, :], mcp[:, 0, :], mcp[:, 1, :], ALU.max).then_inc(c_chain, 1)
                            wait(dve, c_turned, tile)
                            dve.wait_ge(c_chain, base + 1)
                            dve.tensor_copy(m3[:, 0, :], mc[:, :]).then_inc(c_chain, 1)
                            dve.wait_ge(c_chain, base + 2)
                            dve.tensor_tensor(mrest[:, :], mc[:, :], m3[:, 0, :], ALU.subtract).then_inc(c_chain, 1)
                            dve.wait_ge(c_chain, base + 3)
                            dve.tensor_copy(m3[:, 1, :], mrest[:, :]).then_inc(c_chain, 1)
                            dve.wait_ge(c_chain, base + 4)
                            dve.tensor_tensor(m3[:, 2, :], mrest[:, :], m3[:, 1, :], ALU.subtract).then_inc(c_chain, 1)
                    if u > 0 and logits:
                        sums(n - 1, u - 1, parity)
                    elif u == 0 and not (isinstance(s, int) and s == 0):
                        sums(n - 1, 3, 1 - parity)
                    if products:
                        for pair in range(2):
                            dve.wait_ge(xa_ready, 8 * s - 8 + 2 * u + pair + 2)
                            eb = 4 * u + 2 * pair
                            dve.tensor_tensor(xacc[:, eb:eb + 2, :],
                                              ps[:, (XACC + pair) * BANK:(XACC + pair + 1) * BANK].rearrange("p (e d) -> p e d", e=2),
                                              xacc[:, eb:eb + 2, :], ALU.add).then_inc(xa_read, 1)
                    if logits and u % 2 == 1:
                        keep_turned(2 * s + u // 2)
            supers(dve, run)


def experts(nc, m, ps, tag, xacc, yt, ew, eb_in):
    RING = 4
    with phase_of(nc, tag) as (ctx, sem, sb):
        w = sb("w", [P, RING, 4, DC, D])
        bias = sb("bias", [P, EB, D])
        xT = sb("xT", [P, DC, SLOTS])
        stats, mv = sb("stats", [P, EB, 6]), sb("mv", [P, EB, 2])
        ve, sdv, rs = sb("ve", [P, EB]), sb("sdv", [P, EB]), sb("rs", [P, EB])
        w_loaded = [sem(f"w_loaded{i}") for i in range(RING)]
        b_loaded = sem("b_loaded")
        clipped, stats_done, mv_done, ve_done = sem("clipped"), sem("stats_done"), sem("mv_done"), sem("ve_done")
        sd_done, rs_done, normed, tanh_done = sem("sd_done"), sem("rs_done"), sem("normed"), sem("tanh_done")
        filled, copied = sem("filled"), sem("copied")
        y_ready, y_kept = sem("y_ready"), sem("y_kept")
        block = ctx.enter_context(nc.Block())

        @block.sync
        def _(sp):
            for b in range(EB):
                if b == 1:
                    for j in range(4):
                        sp.dma_start(bias[32 * j:32 * j + 32, :, :],
                                     eb_in.rearrange("(b j) d -> j b d", j=4)[j, :, :].partition_broadcast(32)).then_inc(b_loaded, 16)
                wait(sp, y_ready, b - RING + 1)
                for j in range(4):
                    sp.dma_start(w[:, b % RING, j, :, :], ew[4 * b + j].rearrange("(c p) h -> p c h", p=P)).then_inc(w_loaded[b % RING], 16)

        @block.vector
        def _(dve):
            dve.tensor_scalar(xacc[:, :, :], xacc[:, :, :], -33000.0, 65000.0, ALU.max, ALU.min).then_inc(clipped, 1)
            dve.wait_ge(clipped, 1)
            for b in range(EB):
                dve.bn_stats(stats[:, b, :], xacc[:, b, :]).then_inc(stats_done, 1)
            for b in range(EB):
                dve.wait_ge(stats_done, b + 1)
                dve.bn_aggr(mv[:, b, :], stats[:, b, :]).then_inc(mv_done, 1)
            dve.wait_ge(mv_done, EB)
            dve.tensor_scalar(ve[:, :], mv[:, :, 1], EPS, None, ALU.add).then_inc(ve_done, 1)
            dve.wait_ge(sd_done, 1)
            dve.reciprocal(rs[:, :], sdv[:, :]).then_inc(rs_done, 1)
            dve.wait_ge(rs_done, 1)
            for b in range(EB):
                dve.tensor_scalar(xacc[:, b, :], xacc[:, b, :], mv[:, b, 0:1], rs[:, b:b + 1],
                                  ALU.subtract, ALU.mult).then_inc(normed, 1)
            for i in range(EB // 4 * DC):
                bg, c = divmod(i, DC)
                dve.wait_ge(filled, i + 1)
                dve.tensor_copy(xT[:, c, bg * BANK:(bg + 1) * BANK], ps[:, (i % 4) * BANK:(i % 4 + 1) * BANK]).then_inc(copied, 1)
            dve.wait_ge(b_loaded, 64)
            for b in range(EB):
                dve.wait_ge(y_ready, b + 1)
                dve.tensor_tensor(yt[:, b, :], ps[:, (4 + b % 4) * BANK:(4 + b % 4) * BANK + D], bias[:, b, :],
                                  ALU.add).then_inc(y_kept, 1)

        @block.scalar
        def _(act):
            act.wait_ge(ve_done, 1)
            act.activation(sdv[:, :], ve[:, :], ACT.Sqrt).then_inc(sd_done, 1)
            for b in range(0, EB, 4):
                act.wait_ge(normed, b + 4)
                act.activation(xacc[:, b:b + 4, :], xacc[:, b:b + 4, :], ACT.Tanh).then_inc(tanh_done, 1)

        @block.tensor
        def _(pe):
            for i in range(EB // 4 * DC):
                bg, c = divmod(i, DC)
                pe.wait_ge(tanh_done, bg + 1)
                wait(pe, copied, i - 3)
                for k in range(4):
                    mm = pe.transpose(ps[:, (i % 4) * BANK + k * P:(i % 4) * BANK + (k + 1) * P],
                                      xacc[:, 4 * bg + k, c * P:(c + 1) * P], m.ident[:, :])
                mm.then_inc(filled, 1)
            pe.wait_ge(copied, EB // 4 * DC)
            for b in range(EB):
                pe.wait_ge(w_loaded[b % RING], 64 * (b // RING + 1))
                wait(pe, y_kept, b - 3)
                for c in range(DC):
                    for j in range(4):
                        n0 = (4 * b + j) * PS
                        mm = pe.matmul(ps[32 * j:32 * j + 32, (4 + b % 4) * BANK:(4 + b % 4) * BANK + D],
                                       xT[:, c, n0:n0 + PS], w[:, b % RING, j, c, :], start=(c == 0), stop=(c == DC - 1))
                mm.then_inc(y_ready, 1)


def combine(nc, m, ps, tag, xlnT, phi, pbcol, mct, yt, out):
    AHEAD = 3
    with phase_of(nc, tag) as (ctx, sem, sb):
        ct = [sb(f"ct{i}", [P, EB, BANK]) for i in range(2)]
        csum = sb("csum", [P, BANK])
        rsum = sb("rsum", [P, BANK])
        LT, Y, SUM = 0, 4, 6

        lt_ready = sem("lt_ready")
        ct_exp = sem("ct_exp")
        added = sem("added")
        sum_ready = sem("sum_ready")
        r_ready = sem("r_ready")
        c_ready = sem("c_ready")
        y_ready = sem("y_ready")
        x_added = sem("x_added")
        stored = sem("stored")
        block = ctx.enter_context(nc.Block())

        def groups(eng, run):
            run(0, 0, True, False)
            with eng.Fori(0, G // 2 - 1) as it:
                run(2 * it + 1, 1, True, True)
                run(2 * it + 2, 0, True, True)
            run(G - 1, 1, True, True)
            run(G, 0, False, True)

        @block.tensor
        def _(pe):
            def run(g, parity, logits, products):
                def logits_t(b):
                    n = EB * g + b
                    wait(pe, ct_exp, n - 3)
                    o = ps[:, (LT + b % 4) * BANK:(LT + b % 4 + 1) * BANK]
                    for c in range(DC):
                        pe.matmul(o, phi[:, c, b * P:(b + 1) * P],
                                  xlnT[:, c:c + 1, bass.ds(g * BANK, BANK)].rearrange("p a n -> p (a n)"),
                                  start=(c == 0), stop=False)
                    pe.matmul(o, m.sameneg[0:3 * PS, :], mct[0:3 * PS, bass.ds(g * BANK, BANK)],
                              start=False, stop=True).then_inc(lt_ready, 1)

                def product(i):
                    zt, quarter = divmod(i, 4)
                    if zt == 0:
                        pe.wait_ge(c_ready, EB * (g - 1) + 4 * quarter + 4)
                    if quarter == 0:
                        pe.wait_ge(x_added, 4 * (g - 1) + zt + 1)
                    for kb in range(4 * quarter, 4 * quarter + 4):
                        mm = pe.matmul(ps[:, (Y + zt % 2) * BANK:(Y + zt % 2) * BANK + D],
                                       ct[1 - parity][:, kb, zt * P:(zt + 1) * P], yt[:, kb, :],
                                       start=(kb == 0), stop=(kb == EB - 1))
                    if quarter == 3:
                        mm.then_inc(y_ready, 1)

                def total():
                    pe.wait_ge(added, (EB - 1) * g + EB - 1)
                    pe.matmul(ps[:, SUM * BANK:(SUM + 1) * BANK], m.same[:, :], csum[:, :],
                              start=True, stop=True).then_inc(sum_ready, 1)

                if logits:
                    for b in range(AHEAD):
                        logits_t(b)
                for i in range(EB):
                    if products:
                        product(i)
                    if logits and i + AHEAD < EB:
                        logits_t(i + AHEAD)
                if logits:
                    total()
            groups(pe, run)

        @block.scalar
        def _(act):
            def run(g, parity, logits, products):
                if not logits:
                    return
                wait(act, y_ready, 4 * g - 3)
                for b in range(EB):
                    act.wait_ge(lt_ready, EB * g + b + 1)
                    act.activation(ct[parity][:, b, :], ps[:, (LT + b % 4) * BANK:(LT + b % 4 + 1) * BANK], ACT.Exp,
                                   bias=pbcol[:, b:b + 1]).then_inc(ct_exp, 1)
            groups(act, run)

        @block.gpsimd
        def _(pool):
            pool.sem_inc(y_ready, 1)
            pool.sem_inc(x_added, 2)

            def run(g, parity, logits, products):
                if not logits:
                    return
                wait(pool, sum_ready, g)
                for b in range(1, EB):
                    n = (EB - 1) * g + b - 1
                    pool.wait_ge(ct_exp, EB * g + b + 1)
                    wait(pool, added, n)
                    pool.tensor_tensor(csum[:, :], ct[parity][:, 0, :] if b == 1 else csum[:, :],
                                       ct[parity][:, b, :], ALU.add).then_inc(added, 1)
            groups(pool, run)

        @block.vector
        def _(dve):
            def run(g, parity, logits, products):
                if not products:
                    return
                dve.wait_ge(sum_ready, g)
                dve.reciprocal(rsum[:, :], ps[:, SUM * BANK:(SUM + 1) * BANK]).then_inc(r_ready, 1)
                dve.wait_ge(r_ready, g)
                for b in range(EB):
                    c = ct[1 - parity][:, b, :]
                    dve.tensor_tensor(c, c, rsum[:, :], ALU.mult).then_inc(c_ready, 1)
                for zt in range(4):
                    n = 4 * (g - 1) + zt
                    dve.wait_ge(y_ready, n + 2)
                    xt = m.x[:, bass.ds(n, 1), :].rearrange("p a d -> p (a d)")
                    dve.tensor_tensor(xt, ps[:, (Y + zt % 2) * BANK:(Y + zt % 2) * BANK + D], xt,
                                      ALU.add).then_inc(x_added, 1)
            groups(dve, run)

        @block.sync
        def _(sp):
            if out is None:
                return
            o = out.rearrange("a (t p) d -> p (a t) d", p=P)

            def run(g, parity, logits, products):
                if products:
                    sp.wait_ge(x_added, 4 * g + 2)
                    sp.dma_start(o[:, bass.ds(4 * (g - 1), 4), :], m.x[:, bass.ds(4 * (g - 1), 4), :]).then_inc(stored, 16)
            groups(sp, run)
            sp.wait_ge(stored, 16 * G)


def cut_bias(nc, m, tag, pb_in, pbcol_in, phi_in, phi, pb3, pbcol):
    with phase_of(nc, tag) as (ctx, sem, sb):
        row, rest = sb("row", [1, SLOTS]), sb("rest", [1, SLOTS])
        parts = sb("parts", [1, 3, SLOTS], BF16)
        loaded, row_loaded, chain, placed = sem("loaded"), sem("row_loaded"), sem("chain"), sem("placed")
        block = ctx.enter_context(nc.Block())

        @block.sync
        def _(sp):
            sp.dma_start(row[:, :], pb_in.rearrange("(a s) -> a s", a=1)).then_inc(row_loaded, 16)
            sp.dma_start(phi[:, :, :], phi_in.rearrange("(c p) e -> p c e", p=P)).then_inc(loaded, 16)
            sp.dma_start(pbcol[:, :], pbcol_in).then_inc(loaded, 16)
            sp.wait_ge(chain, 4)
            for part in range(3):
                sp.dma_start(pb3[part:part + 1, :], parts[:, part, :]).then_inc(placed, 16)
            sp.wait_ge(placed, 48)
            sp.wait_ge(loaded, 32)

        @block.vector
        def _(dve):
            dve.wait_ge(row_loaded, 16)
            dve.tensor_copy(parts[:, 0, :], row[:, :]).then_inc(chain, 1)
            dve.wait_ge(chain, 1)
            dve.tensor_tensor(rest[:, :], row[:, :], parts[:, 0, :], ALU.subtract).then_inc(chain, 1)
            dve.wait_ge(chain, 2)
            dve.tensor_copy(parts[:, 1, :], rest[:, :]).then_inc(chain, 1)
            dve.wait_ge(chain, 3)
            dve.tensor_tensor(parts[:, 2, :], rest[:, :], parts[:, 1, :], ALU.subtract).then_inc(chain, 1)


def build(nc, t, out):
    with ExitStack() as ctx:
        sb = lambda n, shape, dt=F32: ctx.enter_context(nc.sbuf_tensor(n, shape, dt))
        ps_t = ctx.enter_context(nc.psum_tensor("ps", [P, 8 * BANK], F32))
        ps = ps_t[:, :]
        m = Kept()
        m.x = sb("x", [P, T, D])
        m.ident, m.identb = sb("ident", [P, P]), sb("identb", [P, P], BF16)
        m.mask_qk = sb("mask_qk", [P, P], BF16)
        m.sel, m.same, m.sameneg = sb("sel", [P, HD + 1]), sb("same", [P, P]), sb("sameneg", [P, P], BF16)
        m.onesb = sb("onesb", [P, P], BF16)
        load_and_constants(nc, m, t["x"])

        def attention_layer(tag, wq, wk, wv, wo, bias, denom_bias):
            parts_q = nc.dram_tensor(f"{tag}_parts_q", (3, D, N), BF16).ap()
            parts_k = nc.dram_tensor(f"{tag}_parts_k", (3, D, N), BF16).ap()
            with nc.sbuf_tensor(f"{tag}_attn", [P, T, D], F32) as attn:
                with nc.sbuf_tensor(f"{tag}_v", [P, T, D], F32) as v:
                    with nc.sbuf_tensor(f"{tag}_xlnT", [P, DC, N], F32) as xlnT:
                        layernorm(nc, m, ps, f"{tag}_ln", attn, xlnT)
                        project_qkv(nc, m, ps, f"{tag}_qkv", xlnT, v, wq, wk, wv, parts_q, parts_k)
                    attention(nc, m, ps, f"{tag}_att", v, attn, parts_q, parts_k, denom_bias)
                project_out(nc, m, ps, f"{tag}_out", attn, wo, bias)

        def mixture_layer(tag, last):
            with ExitStack() as c2:
                sb2 = lambda n, shape, dt=F32: c2.enter_context(nc.sbuf_tensor(f"{tag}_{n}", shape, dt))
                xlnT, xacc = sb2("xlnT", [P, DC, N]), sb2("xacc", [P, EB, D])
                phi, pb3 = sb2("phi", [P, DC, SLOTS]), sb2("pb3", [3, SLOTS], BF16)
                mct, pbcol = sb2("mct", [3 * PS, N], BF16), sb2("pbcol", [P, EB])
                cut_bias(nc, m, f"{tag}_pb", t["phi_b"], t["phi_bT"], t["phi_wT"], phi, pb3, pbcol)
                with nc.sbuf_tensor(f"{tag}_xln", [P, T, D], F32) as xln:
                    layernorm(nc, m, ps, f"{tag}_ln", xln, xlnT)
                    dispatch(nc, m, ps, f"{tag}_disp", xln, xlnT, phi, pb3, xacc, mct)
                with nc.sbuf_tensor(f"{tag}_yt", [P, EB, D], F32) as yt:
                    experts(nc, m, ps, f"{tag}_exp", xacc, yt, t["expert_w"], t["expert_b"])
                    combine(nc, m, ps, f"{tag}_comb", xlnT, phi, pbcol, mct, yt, out if last else None)

        attention_layer("a", t["a_WqT"], t["a_WkT"], t["a_WvT"], t["a_WoT"], t["a_bo"], t["a_db"])
        mixture_layer("f", False)
        attention_layer("b", t["b_WqT"], t["b_WkT"], t["b_WvT"], t["b_WoT"], None, None)
        mixture_layer("g", True)


def kernel(**inputs):
    import numpy as _np
    import concourse.bacc as _bacc
    from concourse import mybir as _mybir
    from concourse.bass_utils import run_bass_kernel_spmd as _run

    arrays = {"x": inputs["L0_attn_a_x"]}
    for short, name in (("q", "Wq"), ("k", "Wk"), ("v", "Wv"), ("o", "Wo")):
        arrays[f"a_W{short}T"] = _np.asarray(inputs[f"L0_attn_a_{name}"]).T
        arrays[f"b_W{short}T"] = _np.asarray(inputs[f"L0_attn_b_{short}_proj_weight"]).T
    arrays["a_bo"] = inputs["L0_attn_a_bo"]
    arrays["a_db"] = inputs["L0_attn_a_denom_bias"]
    arrays["phi_wT"] = _np.asarray(inputs["L0_ffn_phi_w"]).T
    arrays["phi_b"] = inputs["L0_ffn_phi_b"]
    arrays["phi_bT"] = _np.asarray(inputs["L0_ffn_phi_b"]).reshape(EB, P).T
    arrays["expert_w"] = inputs["L0_ffn_expert_w"]
    arrays["expert_b"] = inputs["L0_ffn_expert_b"]

    nc = _bacc.Bacc("TRN2", target_bir_lowering=False, num_devices=1)
    given, t = {}, {}
    for name, a in arrays.items():
        a = _np.ascontiguousarray(a)
        given[f"in_{name}"] = a
        t[name] = nc.dram_tensor(f"in_{name}", a.shape, _mybir.dt.from_np(a.dtype), kind="ExternalInput").ap()
    out = nc.dram_tensor("out", (1, N, D), _mybir.dt.float32, kind="ExternalOutput").ap()
    build(nc, t, out)
    r = _run(nc, [given], core_ids=[0])
    return r.results[0]["out"]
```

```python
from contextlib import ExitStack, contextmanager

import concourse.bass as bass
from concourse import mybir

F32 = mybir.dt.float32
BF16 = mybir.dt.bfloat16
F16 = mybir.dt.float16
U32 = mybir.dt.uint32
ALU = mybir.AluOpType
ACT = mybir.ActivationFunctionType
AX = mybir.AxisListType

P = 128
N, D = 4096, 256
T = N // P
DC = D // P
HEADS, HD = 16, 16
SCALE = float(HD) ** -0.5
EPS = 1e-5
NEG = -3.0e38
BANK = 512
TERMS_Q = (0, 1, 0, 1, 2, 0)
TERMS_K = (0, 0, 1, 1, 0, 2)
ROWS = HD * len(TERMS_Q)
ROWS_M = ROWS + 3
VW = 32
G = N // BANK
KB = BANK // P
SLOTS, NE, PS = 2048, 64, 32
EB = SLOTS // P
XLN_SCALE = 256.0
D_SCALE = 2.0 ** 14
TOP = 2.0 ** 14
TERMS = tuple((i, j, c) for i, j in ((0, 0), (0, 1), (1, 0)) for c in range(DC))


class Kept:
    pass


@contextmanager
def phase_of(nc, tag):
    sems = []

    def sem(name):
        sems.append(nc.alloc_semaphore(f"{tag}_{name}"))
        return sems[-1]

    with ExitStack() as ctx:
        yield ctx, sem, lambda name, shape, dt=F32: ctx.enter_context(nc.sbuf_tensor(f"{tag}_{name}", shape, dt))
    nc.clear_and_free_semaphores(sems)
    nc.all_engine_barrier(sem_only=True)


def wait(eng, sem, value):
    if isinstance(value, int) and value <= 0:
        return
    eng.wait_ge(sem, value)


class Scales:

    def __init__(self, sb, name):
        self.top, self.bottom, self.spread = sb(f"{name}_top", [P, 1]), sb(f"{name}_bottom", [P, 1]), sb(f"{name}_spread", [P, P])
        self.largest, self.power, self.inverse = (sb(f"{name}_{n}", [P, 1]) for n in ("largest", "power", "inverse"))
        self.scale, self.back = sb(f"{name}_scale", [P, 1]), sb(f"{name}_back", [P, 1])

    def make(self, dve, flat, gathered_at, chain, gathered):
        dve.tensor_reduce(self.top[:, :], flat, AX.X, ALU.max).then_inc(chain, 1)
        dve.tensor_reduce(self.bottom[:, :], flat, AX.X, ALU.min).then_inc(chain, 1)
        dve.wait_ge(chain, 2)
        dve.scalar_tensor_tensor(self.largest[:, :], self.bottom[:, :], -1.0, self.top[:, :], ALU.mult, ALU.max).then_inc(chain, 1)
        dve.wait_ge(chain, 3)
        dve.tensor_copy(self.spread[:, :], self.largest[:, :].broadcast_to([P, P])).then_inc(chain, 1)
        dve.wait_ge(gathered, 1)
        dve.tensor_reduce(self.top[:, :], gathered_at, AX.X, ALU.max).then_inc(chain, 1)
        dve.wait_ge(chain, 5)
        dve.tensor_scalar(self.largest[:, :], self.top[:, :], 2.0 ** -60, 2.0 ** 120, ALU.max, ALU.min).then_inc(chain, 1)
        dve.wait_ge(chain, 6)
        dve.tensor_scalar(self.power[:, :].bitcast(U32), self.largest[:, :].bitcast(U32), 0x7F800000, None,
                          ALU.bitwise_and).then_inc(chain, 1)
        dve.wait_ge(chain, 7)
        dve.reciprocal(self.inverse[:, :], self.power[:, :]).then_inc(chain, 1)
        dve.wait_ge(chain, 8)
        return 8

    def gather(self, pe, m, at, chain, gathered):
        pe.wait_ge(chain, 4)
        pe.matmul(at, self.spread[:, :], m.ident[:, :], start=True, stop=True).then_inc(gathered, 1)

    def cut(self, dve, flat, parts, done):
        dve.tensor_scalar(parts[:, 0, :], flat, self.scale[:, 0:1], None, ALU.mult).then_inc(done, 1)
        dve.wait_ge(done, 1)
        dve.scalar_tensor_tensor(parts[:, 1, :], flat, self.scale[:, 0:1], parts[:, 0, :],
                                 ALU.mult, ALU.subtract).then_inc(done, 1)


def load_and_cut(nc, m, ps, x_in, phi_in, pb_in, phi_parts, pb_parts):
    with phase_of(nc, "cut") as (ctx, sem, sb):
        phi, parts = sb("phi", [P, DC, SLOTS]), sb("parts", [P, 2, DC, SLOTS], F16)
        row, rest = sb("row", [1, SLOTS]), sb("rest", [1, SLOTS])
        bparts = sb("bparts", [1, 3, SLOTS], BF16)
        scales, bscale = Scales(sb, "phi"), sb("bscale", [P, 1])
        loaded, row_loaded, x_loaded = sem("loaded"), sem("row_loaded"), sem("x_loaded")
        cleared, built = sem("cleared"), sem("built")
        chain = sem("chain")
        gathered = sem("gathered")
        phi_cut = sem("phi_cut")
        row_cut = sem("row_cut")
        stored = sem("stored")
        block = ctx.enter_context(nc.Block())
        phi_f, parts_f = phi[:, :, :].rearrange("p c e -> p (c e)"), parts[:, :, :, :].rearrange("p i c e -> p i (c e)")

        @block.sync
        def _(sp):
            sp.dma_start(phi[:, :, :], phi_in.rearrange("(c p) e -> p c e", p=P)).then_inc(loaded, 16)
            sp.dma_start(row[:, :], pb_in.rearrange("(a s) -> a s", a=1)).then_inc(row_loaded, 16)
            sp.dma_start(m.x[:, :, :], x_in.rearrange("a (t p) d -> p (a t) d", p=P)).then_inc(x_loaded, 16)
            for part in range(2):
                sp.wait_ge(phi_cut, part + 1)
                sp.dma_start(phi_parts[part], parts[:, part, :, :]).then_inc(stored, 16)
            sp.wait_ge(row_cut, 6)
            sp.dma_start(pb_parts, bparts[:, :, :]).then_inc(stored, 16)
            sp.wait_ge(stored, 48)
            sp.wait_ge(x_loaded, 16)

        @block.gpsimd
        def _(pool):
            pool.wait_ge(cleared, 1)
            for t in (m.ident, m.identb):
                pool.affine_select(out=t[:, :], in_=t[:, :], pattern=[[-1, P]], compare_op=ALU.not_equal,
                                   fill=1.0, base=0, channel_multiplier=1)
            pool.affine_select(out=m.mask_qk[:, :], in_=m.mask_qk[:, :], pattern=[[-1, P]],
                               compare_op=ALU.is_ge, fill=NEG, base=0, channel_multiplier=1).then_inc(built, 1)
            n = 1
            for j in range(4):
                for t, pattern, fill in ((m.sel[:, :], [[-1, HD + 1]], 1.0),
                                         (m.same[:, :].rearrange("p (a c) -> p a c", a=4), [[0, 4], [-1, 32]], 1.0),
                                         (m.sameneg[:, :].rearrange("p (a c) -> p a c", a=4), [[0, 4], [-1, 32]], -1.0)):
                    pool.wait_ge(built, n)
                    pool.affine_select(out=t, in_=t, pattern=pattern, compare_op=ALU.not_equal,
                                       fill=fill, base=-32 * j, channel_multiplier=1).then_inc(built, 1)
                    n += 1
            pool.wait_ge(built, n)

        @block.tensor
        def _(pe):
            pe.wait_ge(built, 1)
            scales.gather(pe, m, ps[:, 0:P], chain, gathered)

        @block.vector
        def _(dve):
            for t in (m.ident, m.identb, m.mask_qk, m.sel, m.same, m.sameneg):
                dve.memset(t[:, :], 0.0)
            dve.memset(m.onesb[:, :], 1.0).then_inc(cleared, 1)
            dve.wait_ge(loaded, 16)
            n = scales.make(dve, phi_f, ps[:, 0:P], chain, gathered)
            dve.tensor_scalar(m.unscale[:, :], scales.power[:, :], 1.0 / (TOP * XLN_SCALE), None, ALU.mult).then_inc(chain, 1)
            dve.tensor_scalar(scales.scale[:, :], scales.inverse[:, :], TOP, None, ALU.mult).then_inc(chain, 1)
            dve.tensor_scalar(bscale[:, :], scales.inverse[:, :], TOP * XLN_SCALE, None, ALU.mult).then_inc(chain, 1)
            dve.wait_ge(chain, n + 3)
            scales.cut(dve, phi_f, parts_f, phi_cut)
            dve.wait_ge(row_loaded, 16)
            dve.tensor_scalar(row[:, :], row[:, :], bscale[0:1, 0:1], None, ALU.mult).then_inc(row_cut, 1)
            dve.wait_ge(row_cut, 1)
            dve.tensor_copy(bparts[:, 0, :], row[:, :]).then_inc(row_cut, 1)
            dve.wait_ge(row_cut, 2)
            dve.tensor_tensor(rest[:, :], row[:, :], bparts[:, 0, :], ALU.subtract).then_inc(row_cut, 1)
            dve.wait_ge(row_cut, 3)
            dve.tensor_copy(bparts[:, 1, :], rest[:, :]).then_inc(row_cut, 1)
            dve.wait_ge(row_cut, 4)
            dve.tensor_tensor(bparts[:, 2, :], rest[:, :], bparts[:, 1, :], ALU.subtract).then_inc(row_cut, 2)
            dve.wait_ge(row_cut, 6)


def transposed(nc, ps, tag, src, dst, after=None):
    jobs = [(tg, c) for tg in range(T // 4) for c in range(DC)]

    def pe_part(pe, ident, ready, filled, act_copied, dve_copied, cut=False):
        for i, (tg, c) in enumerate(jobs):
            ready(pe, 4 * tg + 4)
            if i >= 4:
                if cut:
                    pe.wait_ge(dve_copied, i - 3)
                else:
                    wait(pe, act_copied if i % 2 == 0 else dve_copied, (i - 4) // 2 + 1)
            for k in range(4):
                mm = pe.transpose(ps[:, (i % 4) * BANK + k * P:(i % 4) * BANK + (k + 1) * P],
                                  src[:, 4 * tg + k, c * P:(c + 1) * P], ident)
            mm.then_inc(filled, 1)

    def copy_part(eng, copy, odd, filled, copied):
        for i, (tg, c) in enumerate(jobs):
            if i % 2 == odd:
                eng.wait_ge(filled, i + 1)
                copy(dst[:, c, tg * BANK:(tg + 1) * BANK], ps[:, (i % 4) * BANK:(i % 4 + 1) * BANK]).then_inc(copied, 1)

    return pe_part, copy_part


def layernorm(nc, m, ps, tag, xln, xlnT, by_token=None, loads=()):
    cut = by_token is not None
    GT = 4
    with phase_of(nc, tag) as (ctx, sem, sb):
        stats, mv = sb("stats", [P, T, 6]), sb("mv", [P, T, 2])
        ve, sd, rs = sb("ve", [P, T]), sb("sd", [P, T]), sb("rs", [P, T])
        stats_done, mv_done, ve_done, sd_done = sem("stats_done"), sem("mv_done"), sem("ve_done"), sem("sd_done")
        rs_done, normed = sem("rs_done"), sem("normed")
        filled, act_copied, dve_copied = sem("filled"), sem("act_copied"), sem("dve_copied")
        token_high, token_low = sem("token_high"), sem("token_low")
        loaded = sem("loaded")
        pe_part, copy_part = transposed(nc, ps, tag, xln, xlnT)
        jobs = [(tg, c) for tg in range(T // 4) for c in range(DC)]
        block = ctx.enter_context(nc.Block())

        def group(t, g):
            return t[:, GT * g:GT * (g + 1)]

        def part_of(part, i):
            tg, c = jobs[i]
            return xlnT[:, part, c, tg * BANK:(tg + 1) * BANK], ps[:, (i % 4) * BANK:(i % 4 + 1) * BANK]

        @block.sync
        def _(sp):
            for dst, src in loads:
                sp.dma_start(dst, src).then_inc(loaded, 16)
            if loads:
                sp.wait_ge(loaded, 16 * len(loads))

        @block.vector
        def _(dve):
            def statistics(g):
                for t in range(GT * g, GT * (g + 1)):
                    dve.bn_stats(stats[:, t, :], m.x[:, t, :]).then_inc(stats_done, 1)
                for t in range(GT * g, GT * (g + 1)):
                    dve.wait_ge(stats_done, t + 1)
                    dve.bn_aggr(mv[:, t, :], stats[:, t, :]).then_inc(mv_done, 1)
                dve.wait_ge(mv_done, GT * (g + 1))
                dve.tensor_scalar(group(ve, g), mv[:, GT * g:GT * (g + 1), 1], EPS, None, ALU.add).then_inc(ve_done, 1)

            def low_part(i):
                dst, bank = part_of(1, i)
                dve.wait_ge(act_copied, i + 1)
                dve.tensor_tensor(dst, bank, part_of(0, i)[0], ALU.subtract).then_inc(dve_copied, 1)

            def normalise(g):
                dve.wait_ge(sd_done, g + 1)
                dve.reciprocal(group(rs, g), group(sd, g)).then_inc(rs_done, 1)
                dve.wait_ge(rs_done, (1 + cut) * g + 1)
                if cut:
                    dve.tensor_scalar(group(rs, g), group(rs, g), XLN_SCALE, None, ALU.mult).then_inc(rs_done, 1)
                    dve.wait_ge(rs_done, 2 * g + 2)
                for t in range(GT * g, GT * (g + 1)):
                    dve.tensor_scalar(xln[:, t, :], m.x[:, t, :], mv[:, t, 0:1], rs[:, t:t + 1],
                                      ALU.subtract, ALU.mult).then_inc(normed, 1)

            def take(g):
                for i in range(DC * g, DC * (g + 1)):
                    if cut:
                        low_part(i)
                    elif i % 2 == 1:
                        dve.wait_ge(filled, i + 1)
                        dve.tensor_copy(xlnT[:, i % DC, g * BANK:(g + 1) * BANK],
                                        ps[:, (i % 4) * BANK:(i % 4 + 1) * BANK]).then_inc(dve_copied, 1)

            GROUPS = T // GT
            statistics(0)
            for g in range(GROUPS):
                if g + 1 < GROUPS:
                    statistics(g + 1)
                normalise(g)
                if g > 0:
                    take(g - 1)
            take(GROUPS - 1)

        @block.scalar
        def _(act):
            def root(g):
                act.wait_ge(ve_done, g + 1)
                act.activation(group(sd, g), group(ve, g), ACT.Sqrt).then_inc(sd_done, 1)
            root(0)
            for g in range(T // GT):
                if g + 1 < T // GT:
                    root(g + 1)
                if cut:
                    act.wait_ge(normed, GT * (g + 1))
                    act.copy(by_token[:, GT * g:GT * (g + 1), 0, :], xln[:, GT * g:GT * (g + 1), :]).then_inc(token_high, 1)
                for i in range(DC * g, DC * (g + 1)):
                    dst, bank = (part_of(0, i) if cut else
                                 (xlnT[:, i % DC, g * BANK:(g + 1) * BANK], ps[:, (i % 4) * BANK:(i % 4 + 1) * BANK]))
                    if cut or i % 2 == 0:
                        act.wait_ge(filled, i + 1)
                        act.copy(dst, bank).then_inc(act_copied, 1)

        @block.gpsimd
        def _(pool):
            if cut:
                for g in range(T // GT):
                    pool.wait_ge(token_high, g + 1)
                    pool.tensor_tensor(by_token[:, GT * g:GT * (g + 1), 1, :], xln[:, GT * g:GT * (g + 1), :],
                                       by_token[:, GT * g:GT * (g + 1), 0, :], ALU.subtract).then_inc(token_low, 1)

        @block.tensor
        def _(pe):
            pe_part(pe, m.ident[:, :], lambda eng, n: eng.wait_ge(normed, n), filled, act_copied, dve_copied, cut)


def project_qkv(nc, m, ps, tag, xlnT, v, wq, wk, wv, parts_q, parts_k):
    HALF = N // 2
    NB = HALF // BANK
    with phase_of(nc, tag) as (ctx, sem, sb):
        w = [sb(f"w{i}", [P, DC, D]) for i in range(3)]
        cut = sb("cut", [P, 2, 3, HALF], BF16)
        rest = sb("rest", [P, 2, BANK])
        w_loaded = [sem(f"w_loaded{i}") for i in range(3)]
        made = sem("made")
        high = sem("high")
        left = sem("left")
        mid = sem("mid")
        low = sem("low")
        stored = [sem("stored0"), sem("stored1")]
        v_made, v_kept = sem("v_made"), sem("v_kept")
        block = ctx.enter_context(nc.Block())
        jobs = [(i, oc, hf) for oc in range(DC) for i in range(2) for hf in range(2)]

        @block.sync
        def _(sp):
            for i, wi in enumerate((wq, wk, wv)):
                sp.dma_start(w[i][:, :, :], wi.rearrange("(c p) o -> p c o", p=P)).then_inc(w_loaded[i], 16)
            for j, (i, oc, hf) in enumerate(jobs):
                sp.wait_ge(low, NB * (j + 1))
                dst = (parts_q, parts_k)[i]
                for part in range(3):
                    sp.dma_start(dst[part, oc * P:(oc + 1) * P, hf * HALF:(hf + 1) * HALF],
                                 cut[:, j % 2, part, :]).then_inc(stored[j % 2], 16)
            for s in stored:
                sp.wait_ge(s, 48 * len(jobs) // 2)

        @block.tensor
        def _(pe):
            n = 0
            for j, (i, oc, hf) in enumerate(jobs):
                if oc == 0 and hf == 0:
                    pe.wait_ge(w_loaded[i], 16)
                for b in range(NB):
                    wait(pe, left, n - 3)
                    for c in range(DC):
                        mm = pe.matmul(ps[:, (n % 4) * BANK:(n % 4 + 1) * BANK], w[i][:, c, oc * P:(oc + 1) * P],
                                       xlnT[:, c, hf * HALF + b * BANK:hf * HALF + (b + 1) * BANK],
                                       start=(c == 0), stop=(c == DC - 1))
                    mm.then_inc(made, 1)
                    n += 1
            pe.wait_ge(w_loaded[2], 16)
            for t in range(T):
                wait(pe, v_kept, t - 3)
                for c in range(DC):
                    mm = pe.matmul(ps[:, (4 + t % 4) * BANK:(4 + t % 4) * BANK + D], xlnT[:, c, t * P:(t + 1) * P],
                                   w[2][:, c, :], start=(c == 0), stop=(c == DC - 1))
                mm.then_inc(v_made, 1)

        @block.scalar
        def _(act):
            n = 0
            for j, (i, oc, hf) in enumerate(jobs):
                scale = SCALE if i == 0 else 1.0
                wait(act, stored[j % 2], 48 * (j // 2))
                for b in range(NB):
                    act.wait_ge(made, n + 1)
                    act.activation(cut[:, j % 2, 0, b * BANK:(b + 1) * BANK], ps[:, (n % 4) * BANK:(n % 4 + 1) * BANK],
                                   ACT.Copy, scale=scale).then_inc(high, 1)
                    act.wait_ge(left, n + 1)
                    act.activation(cut[:, j % 2, 1, b * BANK:(b + 1) * BANK], rest[:, n % 2, :],
                                   ACT.Copy).then_inc(mid, 1)
                    n += 1
            for t in range(T):
                act.wait_ge(v_made, t + 1)
                act.activation(v[:, t, :], ps[:, (4 + t % 4) * BANK:(4 + t % 4) * BANK + D], ACT.Copy).then_inc(v_kept, 1)

        @block.vector
        def _(dve):
            n = 0
            for j, (i, oc, hf) in enumerate(jobs):
                scale = SCALE if i == 0 else 1.0
                for b in range(NB):
                    dve.wait_ge(high, n + 1)
                    wait(dve, low, n - 1)
                    dve.scalar_tensor_tensor(rest[:, n % 2, :], ps[:, (n % 4) * BANK:(n % 4 + 1) * BANK], scale,
                                             cut[:, j % 2, 0, b * BANK:(b + 1) * BANK],
                                             ALU.mult, ALU.subtract).then_inc(left, 1)
                    dve.wait_ge(left, n + 1)
                    dve.wait_ge(mid, n + 1)
                    dve.tensor_tensor(cut[:, j % 2, 2, b * BANK:(b + 1) * BANK], rest[:, n % 2, :],
                                      cut[:, j % 2, 1, b * BANK:(b + 1) * BANK], ALU.subtract).then_inc(low, 1)
                    n += 1


def chunks():
    out = []
    for t in range(T):
        last = t // 4
        for c in range(last + 1):
            out.append((t, c, BANK if c < last else P * (t % 4 + 1), c == last))
    return out


HALF_T = T // 2
CUTS = 5
CHUNKS = chunks()
CHUNKS_A = sum(t < HALF_T for t, _, _, _ in CHUNKS)
FIRST_ITEMS = CHUNKS[:CHUNKS_A + 4] + ["A"] + CHUNKS[CHUNKS_A + 4:]
ITEMS = FIRST_ITEMS[:4] + ["B"] + FIRST_ITEMS[4:]
N_FIRST, N_ITEMS = len(FIRST_ITEMS), len(ITEMS)
STEPS = [(g, c) for g in range(G) for c in range(g + 1)]
TAIL_ITEMS = 8
ITEMS_BY = [(N_ITEMS - TAIL_ITEMS) * (s + 1) // len(STEPS) for s in range(len(STEPS))]
RING = 3


def attention(nc, m, ps, tag, v, attn, parts_q, parts_k, denom_bias):
    NS = len(STEPS)
    with phase_of(nc, tag) as (ctx, sem, sb):
        q1 = [sb(f"q1_{i}", [P, N], BF16) for i in range(2)]
        k1 = [sb(f"k1_{i}", [P, N], BF16) for i in range(2)]
        q2 = [sb(f"q2_{i}", [P, N], BF16) for i in range(2)]
        k2 = [sb(f"k2_{i}", [P, N], BF16) for i in range(2)]
        vh = [sb(f"vh_{i}", [P, T, VW]) for i in range(2)]
        pt = sb("pt", [P, 2 * KB, BANK])
        osb = sb("osb", [P, 2, BANK])
        mx = sb("mx", [P, T, G])
        mfull = sb("mfull", [P, HALF_T])
        mrest = sb("mrest", [P, HALF_T])
        m3all = sb("m3", [P, P], BF16)
        m3 = m3all[:, 0:3 * HALF_T].rearrange("p (a t) -> p a t", a=3)
        mt = [sb(f"mt_{i}", [3 * HALF_T, P], BF16) for i in range(2)]
        den = sb("den", [P, HALF_T])
        rden = sb("rden", [P, HALF_T])
        dbias = sb("dbias", [P, HEADS])

        SCORES_T, SCORES = 0, RING
        OUT = ps[:, 6 * BANK:7 * BANK]
        TURNED = ps[:, 7 * BANK:7 * BANK + HALF_T * (HD + 1)].rearrange("p (t c) -> p t c", c=HD + 1)

        set_up = sem("set_up")
        db_loaded, db_ready = sem("db_loaded"), sem("db_ready")
        p1_loaded = [sem("p1_loaded0"), sem("p1_loaded1")]
        p2_loaded = [sem("p2_loaded0"), sem("p2_loaded1")]
        v_ready = sem("v_ready")
        s1_ready, s1_read = sem("s1_ready"), sem("s1_read")
        m_chain = sem("m_chain")
        mt_ready = sem("mt_ready")
        m_placed = [sem("m_placedA"), sem("m_placedB")]
        st_ready = sem("st_ready")
        pt_ready = sem("pt_ready")
        turns = sem("turns")
        masked = sem("masked")
        pv_done = sem("pv_done")
        o_copied = sem("o_copied")
        turned = sem("turned")
        t_read = sem("t_read")
        d_chain = sem("d_chain")
        block = ctx.enter_context(nc.Block())

        LOADS = 16 * 2 * len(TERMS_Q)

        def first_item(h):
            return N_FIRST + N_ITEMS * h

        def bank_of(n, first):
            return (SCORES + (n + N_ITEMS - N_FIRST if first else n) % RING) * BANK

        def phases(eng, phase):
            with eng.Fori(0, HEADS // 2 - 1) as it:
                for parity in range(2):
                    phase(it, parity, True)
            phase(HEADS // 2 - 1, 0, True)
            phase(HEADS // 2 - 1, 1, False)

        @block.sync
        def _(sp):
            def load(q, k, h, loaded):
                for dst, src, terms in ((q, parts_q, TERMS_Q), (k, parts_k, TERMS_K)):
                    for r, part in enumerate(terms):
                        sp.dma_start(dst[r * HD:(r + 1) * HD, :], src[part, bass.ds(h * HD, HD), :]).then_inc(loaded, 16)

            def place(half, parity):
                for part in range(3):
                    sp.dma_start(q2[parity][ROWS + part:ROWS + part + 1, half * N // 2:(half + 1) * N // 2],
                                 mt[half][part * HALF_T:(part + 1) * HALF_T, :]).then_inc(m_placed[half], 16)

            if denom_bias is not None:
                sp.dma_start(dbias[:, :], denom_bias.rearrange("a h b c -> (a b c) h").partition_broadcast(P)
                             ).then_inc(db_loaded, 16)
            load(q1[0], k1[0], 0, p1_loaded[0])
            load(q2[0], k2[0], 0, p2_loaded[0])
            load(q1[1], k1[1], 1, p1_loaded[1])
            sp.wait_ge(mt_ready, 1)
            sp.wait_ge(set_up, 1)
            place(0, 0)

            def phase(it, parity, more):
                h = 2 * it + parity
                if more:
                    sp.wait_ge(st_ready, KB * NS * h + 1)
                    load(q2[1 - parity], k2[1 - parity], h + 1, p2_loaded[1 - parity])
                    if not (isinstance(h, int) and h == HEADS - 2):
                        sp.wait_ge(s1_ready, first_item(h))
                        load(q1[parity], k1[parity], h + 2, p1_loaded[parity])
                sp.wait_ge(mt_ready, 2 * h + 2)
                place(1, parity)
                if more:
                    sp.wait_ge(mt_ready, 2 * h + 3)
                    place(0, 1 - parity)
            phases(sp, phase)
            for s in m_placed:
                sp.wait_ge(s, 48 * HEADS)

        @block.gpsimd
        def _(pool):
            for s, n in ((st_ready, 1), (pt_ready, RING), (pv_done, 2), (o_copied, 1), (turned, 2), (t_read, 1)):
                pool.sem_inc(s, n)
            pool.wait_ge(set_up, 1)
            pool.tensor_copy(vh[0][:, :, 0:HD], v[:, :, 0:HD]).then_inc(v_ready, 1)

            def phase(it, parity, more):
                h = 2 * it + parity
                if more:
                    pool.wait_ge(pv_done, NS * h + 2)
                    pool.tensor_copy(vh[1 - parity][:, :, 0:HD], v[:, :, bass.ds((h + 1) * HD, HD)]).then_inc(v_ready, 1)
                for g in range(G):
                    s = STEPS.index((g, g))
                    for j in range(KB):
                        pool.wait_ge(pt_ready, KB * (NS * h + s) + j + 1 + RING)
                        pool.sem_inc(turns, 1)
                        block_p = pt[:, KB * (s % 2) + j, 0:P]
                        pool.affine_select(out=block_p, in_=block_p, pattern=[[1, P]], compare_op=ALU.is_ge,
                                           fill=0.0, base=0, channel_multiplier=-1).then_inc(masked, 1)
            phases(pool, phase)

        @block.tensor
        def _(pe):
            def item(what, i, lag, bank, q, k, chain):
                wait(pe, s1_read, i - lag + 1)
                if what in ("A", "B"):
                    pe.wait_ge(m_chain, chain)
                    pe.transpose(ps[:, bank:bank + P // 2].bitcast(BF16), m3all[:, :], m.identb[:, :]).then_inc(s1_ready, 1)
                    return
                t, c, width, diag = what
                mm = pe.matmul(ps[:, bank:bank + width], q[0:ROWS, t * P:(t + 1) * P],
                               k[0:ROWS, c * BANK:c * BANK + width], start=True, stop=not diag)
                if diag:
                    mm = pe.matmul(ps[:, bank + width - P:bank + width], m.identb[:, :], m.mask_qk[:, :],
                                   start=False, stop=True)
                mm.then_inc(s1_ready, 1)

            pe.wait_ge(p1_loaded[0], LOADS)
            for i, what in enumerate(FIRST_ITEMS):
                item(what, i, RING, bank_of(i, True), q1[0], k1[0], CUTS)
            pe.wait_ge(set_up, 1)

            def phase(it, parity, more):
                h = 2 * it + parity
                q, k = q2[parity], k2[parity]
                items = ITEMS if more else ["B"]
                done = [0]

                def run_items(upto):
                    for n in range(done[0], min(upto, len(items))):
                        item(items[n], first_item(h) + n, 2 if n < 2 else RING, bank_of(n, False), q1[1 - parity], k1[1 - parity],
                             2 * CUTS * h + (3 * CUTS if items[n] == "A" else 2 * CUTS))
                        done[0] = n + 1

                def scores_t(s, j):
                    g, c = STEPS[s]
                    kb, width = KB * c + j, BANK - P * j if c == g else BANK
                    bank = (SCORES_T + (KB * s + j) % RING) * BANK
                    pe.wait_ge(pt_ready, KB * (NS * h + s) + j + 1)
                    pe.matmul(ps[:, bank:bank + width], k[0:ROWS_M, kb * P:(kb + 1) * P],
                              q[0:ROWS_M, (g + 1) * BANK - width:(g + 1) * BANK],
                              start=True, stop=True).then_inc(st_ready, 1)

                def p_v(s):
                    g, c = STEPS[s]
                    if c == g:
                        pe.wait_ge(masked, KB * (G * h + g) + KB)
                    else:
                        pe.wait_ge(pt_ready, KB * (NS * h + s) + KB + RING)
                    if c == 0:
                        pe.wait_ge(o_copied, G * h + g + 1)
                    for j in range(KB):
                        width = BANK - P * j if c == g else BANK
                        mm = pe.matmul(OUT[32 * j:32 * j + VW, BANK - width:BANK], vh[parity][:, KB * c + j, :],
                                       pt[:, KB * (s % 2) + j, 0:width], start=(c == 0), stop=(c == g))
                    mm.then_inc(pv_done, 1)

                def turn(g):
                    pe.wait_ge(o_copied, G * h + g + 2)
                    if g % 4 == 0:
                        pe.wait_ge(t_read, 2 * h + g // 4 + 1)
                    for k4 in range(4):
                        rows = P if g else 32 * (k4 + 1)
                        mm = pe.matmul(TURNED[:, 4 * (g % 4) + k4, :], osb[0:rows, g % 2, k4 * P:(k4 + 1) * P],
                                       m.sel[0:rows, :], start=True, stop=True)
                    mm.then_inc(turned, 1)

                pe.wait_ge(p2_loaded[parity], LOADS * (it + 1))
                pe.wait_ge(m_placed[0], 48 * (h + 1))
                pe.wait_ge(v_ready, h + 1)
                if more:
                    pe.wait_ge(p1_loaded[1 - parity], LOADS * (it + 1 + parity))
                for s, (g, c) in enumerate(STEPS):
                    if g == G // 2 and c == 0:
                        pe.wait_ge(m_placed[1], 48 * (h + 1))
                    before = ITEMS_BY[s - 1] if s else 0
                    for j in range(KB):
                        scores_t(s, j)
                        run_items(before + (ITEMS_BY[s] - before) * (j + 1) // KB)
                    if s >= 2 and STEPS[s - 2][0] == STEPS[s - 2][1]:
                        turn(STEPS[s - 2][0])
                    if s:
                        p_v(s - 1)
                run_items(N_ITEMS - TAIL_ITEMS // 2)
                p_v(NS - 1)
                run_items(N_ITEMS)
                turn(G - 1)
            phases(pe, phase)

        @block.scalar
        def _(act):
            if denom_bias is not None:
                act.wait_ge(db_loaded, 16)
                act.activation(dbias[:, :], dbias[:, :], ACT.Exp).then_inc(db_ready, 1)

            def phase(it, parity, more):
                h = 2 * it + parity

                def copy_group(g):
                    act.wait_ge(pv_done, NS * h + (g + 1) * (g + 2) // 2 + 2)
                    act.wait_ge(turned, G * h + g + 1)
                    if g:
                        last = act.activation(osb[:, g % 2, :], OUT, ACT.Copy)
                    else:
                        for j in range(KB):
                            last = act.activation(osb[32 * j:32 * j + VW, 0, P * j:BANK],
                                                  OUT[32 * j:32 * j + VW, P * j:BANK], ACT.Copy)
                    last.then_inc(o_copied, 1)

                for s, (g, c) in enumerate(STEPS):
                    act.wait_ge(pv_done, NS * h + s + 1)
                    for j in range(KB):
                        bank = (SCORES_T + (KB * s + j) % RING) * BANK
                        width = BANK - P * j if c == g else BANK
                        act.wait_ge(st_ready, KB * (NS * h + s) + j + 2)
                        act.activation(pt[:, KB * (s % 2) + j, 0:width], ps[:, bank:bank + width], ACT.Exp).then_inc(pt_ready, 1)
                        if j == 1 and s >= 2 and STEPS[s - 2][0] == STEPS[s - 2][1]:
                            copy_group(STEPS[s - 2][0])
                copy_group(G - 1)
            phases(act, phase)

        @block.vector
        def _(dve):
            dve.memset(mx[:, :, :], NEG)
            for i in range(2):
                dve.memset(k2[i][ROWS:ROWS_M, :], -1.0)
                dve.memset(vh[i][:, :, HD + 1:VW], 0.0)
                dve.memset(vh[i][:, :, HD:HD + 1], 1.0)
            dve.memset(m3all[:, :], 0.0).then_inc(set_up, 1)
            dve.wait_ge(set_up, 1)

            def item(what, i, bank):
                dve.wait_ge(s1_ready, i + 1)
                if what in ("A", "B"):
                    half = "AB".index(what)
                    dve.tensor_copy(mt[half][:, :], ps[0:3 * HALF_T, bank:bank + P // 2].bitcast(BF16)).then_inc(s1_read, 1)
                    dve.wait_ge(s1_read, i + 1)
                    dve.sem_inc(mt_ready, 1)
                    return
                t, c, width, _ = what
                dve.tensor_reduce(mx[:, t, c:c + 1], ps[:, bank:bank + width], AX.X, ALU.max).then_inc(s1_read, 1)

            def cut_maxima(half, i, base):
                dve.wait_ge(s1_read, i + 1)
                dve.tensor_reduce(mfull[:, :], mx[:, half * HALF_T:(half + 1) * HALF_T, 0:(half + 1) * G // 2],
                                  AX.X, ALU.max).then_inc(m_chain, 1)
                dve.wait_ge(m_chain, base + 1)
                dve.tensor_copy(m3[:, 0, :], mfull[:, :]).then_inc(m_chain, 1)
                dve.wait_ge(m_chain, base + 2)
                dve.tensor_tensor(mrest[:, :], mfull[:, :], m3[:, 0, :], ALU.subtract).then_inc(m_chain, 1)
                dve.wait_ge(m_chain, base + 3)
                dve.tensor_copy(m3[:, 1, :], mrest[:, :]).then_inc(m_chain, 1)
                dve.wait_ge(m_chain, base + 4)
                dve.tensor_tensor(m3[:, 2, :], mrest[:, :], m3[:, 1, :], ALU.subtract).then_inc(m_chain, 1)

            for i, what in enumerate(FIRST_ITEMS):
                item(what, i, bank_of(i, True))
                if i == CHUNKS_A - 1:
                    cut_maxima(0, i, 0)
            cut_maxima(1, N_FIRST - 1, CUTS)
            if denom_bias is not None:
                dve.wait_ge(db_ready, 1)

            def phase(it, parity, more):
                h = 2 * it + parity
                items = ITEMS if more else ["B"]
                done = [0]

                def run_items(upto):
                    for n in range(done[0], min(upto, len(items))):
                        item(items[n], first_item(h) + n, bank_of(n, False))
                        if n == CHUNKS_A:
                            cut_maxima(0, first_item(h) + n, 2 * CUTS * h + 2 * CUTS)
                        done[0] = n + 1

                def divide(half):
                    ops = 1 if denom_bias is None else 2
                    base = ops * (2 * h + half)
                    dve.wait_ge(turned, G * h + 4 * half + 4 + 2)
                    source = TURNED[:, :, HD]
                    if denom_bias is not None:
                        dve.tensor_scalar(den[:, :], source, dbias[:, bass.ds(h, 1)], None, ALU.add).then_inc(d_chain, 1)
                        dve.wait_ge(d_chain, base + 1)
                        source = den[:, :]
                    dve.reciprocal(rden[:, :], source).then_inc(d_chain, 1)
                    dve.wait_ge(d_chain, base + ops)
                    dve.tensor_tensor(attn[:, half * HALF_T:(half + 1) * HALF_T, bass.ds(h * HD, HD)],
                                      TURNED[:, :, 0:HD],
                                      rden[:, :].unsqueeze(2).broadcast_to([P, HALF_T, HD]), ALU.mult).then_inc(t_read, 1)

                run_items(ITEMS_BY[12])
                divide(0)
                run_items(N_ITEMS)
                if more:
                    cut_maxima(1, first_item(h) + N_ITEMS - 1, 2 * CUTS * h + 3 * CUTS)
                divide(1)
            phases(dve, phase)


def project_out(nc, m, ps, tag, attn, wo, bias):
    with phase_of(nc, tag) as (ctx, sem, sb):
        attnT = sb("attnT", [P, DC, N])
        w = sb("w", [P, DC, D])
        brow = sb("brow", [P, D])
        w_loaded, b_loaded = sem("w_loaded"), sem("b_loaded")
        filled, act_copied, dve_copied = sem("filled"), sem("act_copied"), sem("dve_copied")
        biased, made, added = sem("biased"), sem("made"), sem("added")
        pe_part, copy_part = transposed(nc, ps, tag, attn, attnT)
        block = ctx.enter_context(nc.Block())

        @block.sync
        def _(sp):
            sp.dma_start(w[:, :, :], wo.rearrange("(c p) o -> p c o", p=P)).then_inc(w_loaded, 16)
            if bias is not None:
                sp.dma_start(brow[:, :], bias.partition_broadcast(P)).then_inc(b_loaded, 16)

        @block.tensor
        def _(pe):
            pe_part(pe, m.ident[:, :], lambda eng, n: None, filled, act_copied, dve_copied)
            pe.wait_ge(w_loaded, 16)
            pe.wait_ge(act_copied, T // 4)
            pe.wait_ge(dve_copied, T // 4)
            for t in range(T):
                wait(pe, added, t - 3)
                for c in range(DC):
                    mm = pe.matmul(ps[:, (4 + t % 4) * BANK:(4 + t % 4) * BANK + D], attnT[:, c, t * P:(t + 1) * P],
                                   w[:, c, :], start=(c == 0), stop=(c == DC - 1))
                mm.then_inc(made, 1)

        @block.scalar
        def _(act):
            copy_part(act, act.copy, 0, filled, act_copied)

        @block.gpsimd
        def _(pool):
            if bias is not None:
                pool.wait_ge(b_loaded, 16)
                for t in range(T):
                    pool.tensor_tensor(m.x[:, t, :], m.x[:, t, :], brow[:, :], ALU.add).then_inc(biased, 1)

        @block.vector
        def _(dve):
            copy_part(dve, dve.tensor_copy, 1, filled, dve_copied)
            for t in range(T):
                if bias is not None:
                    dve.wait_ge(biased, t + 1)
                dve.wait_ge(made, t + 1)
                dve.tensor_tensor(m.x[:, t, :], ps[:, (4 + t % 4) * BANK:(4 + t % 4) * BANK + D], m.x[:, t, :],
                                  ALU.add).then_inc(added, 1)


def dispatch(nc, m, ps, tag, xtok, xlnT, phi, pb3, xacc, mct):
    SUPERS = T // 2
    UNIT = SLOTS // 2
    UN = UNIT // PS
    with phase_of(nc, tag) as (ctx, sem, sb):
        shifted = sb("shifted", [P, 2, UNIT])
        ex = sb("ex", [P, 4, UNIT])
        disp = [sb(f"disp{i}", [P, 4, 2, UNIT], F16) for i in range(2)]
        md = sb("md", [P, 2, UN])
        sd = sb("sd", [P, 2, UN])
        rd, rds = sb("rd", [P, 2, UN]), sb("rds", [P, 2, UN])
        mcp = sb("mcp", [P, 2, PS])
        mc = sb("mc", [P, PS])
        mrest = sb("mrest", [P, PS])
        m3 = sb("m3", [P, 3, PS], BF16)
        LOGITS, XACC, TURN = 0, 4, 6

        cleared = sem("cleared")
        l_ready = sem("l_ready")
        sub_done = sem("sub_done")
        md_done = sem("md_done")
        e_done = sem("e_done")
        sum_done = sem("sum_done")
        r_scaled = sem("r_scaled")
        d_made = sem("d_made")
        high = sem("high")
        d_ready = sem("d_ready")
        xa_ready = sem("xa_ready")
        xa_read = sem("xa_read")
        c_chain = sem("c_chain")
        c_turned = sem("c_turned")
        c_kept = sem("c_kept")
        block = ctx.enter_context(nc.Block())

        def supers(eng, run):
            for s in range(2):
                for u in range(4):
                    run(s, s, u)
            with eng.Fori(0, SUPERS // 2 - 1) as it:
                for parity in range(2):
                    for u in range(4):
                        run(2 * it + 2 + parity, parity, u)
            for u in range(5):
                run(SUPERS, 0, u)

        def logits_in(s):
            return not (isinstance(s, int) and s == SUPERS)

        def products_in(s, u):
            return not (isinstance(s, int) and s - 1 - (u == 0) < 0)

        def turns(s, u):
            return u in (0, 2) and not (isinstance(s, int) and (2 * s + u // 2 == 0 or 2 * s + u // 2 > 2 * SUPERS))

        @block.scalar
        def _(act):
            def run(s, parity, u):
                n = 4 * s + u
                if logits_in(s):
                    act.wait_ge(sub_done, n + 1)
                    wait(act, d_ready, n - 3)
                    act.activation(ex[:, u, :], shifted[:, u % 2, :], ACT.Exp, scale=m.unscale[:, 0:1]).then_inc(e_done, 1)
                if u < 4 and (logits_in(s) or u == 0) and not (isinstance(n, int) and n == 0):
                    v, p = (u - 1) % 4, parity if u else 1 - parity
                    base = 5 * (2 * s + u // 2)
                    if u % 2 == 1:
                        wait(act, c_turned, 2 * s + u // 2)
                        act.wait_ge(c_chain, base + 1)
                        act.copy(m3[:, 0, :], mc[:, :]).then_inc(c_chain, 1)
                    act.wait_ge(sum_done, 2 * n)
                    wait(act, d_made, n - 2)
                    act.activation(rds[:, v % 2, :], rd[:, v % 2, :], ACT.Copy, scale=D_SCALE).then_inc(r_scaled, 1)
                    if u % 2 == 1:
                        act.wait_ge(c_chain, base + 3)
                        act.copy(m3[:, 1, :], mrest[:, :]).then_inc(c_chain, 1)
                    wait(act, xa_ready, 8 * (s if u else s - 1) - (12 if v % 2 == 0 else 8))
                    act.wait_ge(d_made, n)
                    act.copy(disp[p][:, v, 0, :], ex[:, v, :]).then_inc(high, 1)
            supers(act, run)

        @block.tensor
        def _(pe):
            def run(s, parity, u):
                n = 4 * s + u
                if logits_in(s):
                    wait(pe, sub_done, n - 1)
                    for b in range(UNIT // BANK):
                        out = ps[:, (LOGITS + 2 * (u % 2) + b) * BANK:(LOGITS + 2 * (u % 2) + b + 1) * BANK]
                        e0 = (u % 2) * UNIT + b * BANK
                        for i, (xp, pp, c) in enumerate(TERMS):
                            pe.matmul(out, xlnT[:, xp:xp + 1, c, bass.ds((2 * s + u // 2) * P, P)].rearrange("p a n -> p (a n)"),
                                      phi[:, pp, c, e0:e0 + BANK], start=(i == 0), stop=False)
                        mm = pe.matmul(out, m.onesb[0:3, :], pb3[0:3, e0:e0 + BANK], start=False, stop=True)
                    mm.then_inc(l_ready, 1)
                if products_in(s, u):
                    quarter, behind, p = ((u - 1) % 4, 1, 1 - parity) if u else (3, 2, parity)
                    if quarter % 2 == 0:
                        pe.wait_ge(d_ready, 4 * s - 1 + quarter // 2)
                    for pair in range(2):
                        k = 8 * s - 10 + 2 * u + pair
                        wait(pe, xa_read, k - 1)
                        for e in range(2):
                            eb = 4 * quarter + 2 * pair + e
                            out = ps[:, (XACC + pair) * BANK + e * D:(XACC + pair) * BANK + (e + 1) * D]
                            for tile in range(2):
                                for i, (dp, xp) in enumerate(((0, 0), (0, 1), (1, 0))):
                                    mm = pe.matmul(out, disp[p][:, 2 * tile + eb // 8, dp, (eb % 8) * P:(eb % 8 + 1) * P],
                                                   xtok[:, bass.ds(2 * (s - behind) + tile, 1), xp, :].rearrange("p a d -> p (a d)"),
                                                   start=(tile == 0 and i == 0), stop=(tile == 1 and i == 2))
                        mm.then_inc(xa_ready, 1)
                if turns(s, u):
                    tile = 2 * s + u // 2 - 1
                    pe.wait_ge(c_chain, 5 * tile + 5)
                    wait(pe, c_kept, tile)
                    pe.transpose(ps[0:3 * PS, TURN * BANK:TURN * BANK + P // 2].bitcast(BF16),
                                 m3[:, :, :].rearrange("p a s -> p (a s)"), m.identb[:, :]).then_inc(c_turned, 1)
            supers(pe, run)

        @block.gpsimd
        def _(pool):
            def run(s, parity, u):
                if not logits_in(s):
                    return
                n = 4 * s + u
                pool.wait_ge(r_scaled, n + 1)
                d = ex[:, u, :].rearrange("p (n q) -> p n q", q=PS)
                pool.tensor_tensor(d, d, rds[:, u % 2, :].unsqueeze(2).broadcast_to([P, UN, PS]), ALU.mult).then_inc(d_made, 1)
                pool.wait_ge(high, n + 1)
                pool.tensor_tensor(disp[parity][:, u, 1, :], ex[:, u, :], disp[parity][:, u, 0, :],
                                   ALU.subtract).then_inc(d_ready, 1)
            supers(pool, run)

        @block.vector
        def _(dve):
            dve.memset(xacc[:, :, :], 0.0).then_inc(cleared, 1)
            dve.wait_ge(cleared, 1)

            def sums(n, u):
                dve.wait_ge(e_done, n + 1)
                dve.tensor_reduce(sd[:, u % 2, :], ex[:, u, :].rearrange("p (n q) -> p n q", q=PS),
                                  AX.X, ALU.add).then_inc(sum_done, 1)
                dve.wait_ge(sum_done, 2 * n + 1)
                wait(dve, r_scaled, n - 1)
                dve.reciprocal(rd[:, u % 2, :], sd[:, u % 2, :]).then_inc(sum_done, 1)

            def keep_turned(tile):
                dve.wait_ge(c_turned, tile + 1)
                dve.tensor_copy(mct[0:3 * PS, bass.ds(tile * P, P)],
                                ps[0:3 * PS, TURN * BANK:TURN * BANK + P // 2].bitcast(BF16)).then_inc(c_kept, 1)

            def run(s, parity, u):
                n = 4 * s + u
                if logits_in(s):
                    at = (LOGITS + 2 * (u % 2)) * BANK
                    l3 = ps[:, at:at + UNIT].rearrange("p (n q) -> p n q", q=PS)
                    dve.wait_ge(l_ready, n + 1)
                    dve.tensor_reduce(md[:, u % 2, :], l3, AX.X, ALU.max).then_inc(md_done, 1)
                    dve.tensor_reduce(mcp[:, u % 2, :], ps[:, at:at + UNIT].rearrange("p (n q) -> p q n", q=PS),
                                      AX.X, ALU.max).then_inc(md_done, 1)
                    dve.wait_ge(md_done, 2 * n + 1)
                    wait(dve, e_done, n - 1)
                    dve.tensor_tensor(shifted[:, u % 2, :].rearrange("p (n q) -> p n q", q=PS), l3,
                                      md[:, u % 2, :].unsqueeze(2).broadcast_to([P, UN, PS]),
                                      ALU.subtract).then_inc(sub_done, 1)
                    if u % 2 == 1:
                        dve.wait_ge(md_done, 2 * n + 2)
                        dve.tensor_tensor(mc[:, :], mcp[:, 0, :], mcp[:, 1, :], ALU.max).then_inc(c_chain, 1)
                if (logits_in(s) or u == 0) and not (isinstance(n, int) and n == 0):
                    sums(n - 1, (u - 1) % 4)
                base = 5 * (2 * s + u // 2)
                if logits_in(s) and u % 2 == 1:
                    dve.wait_ge(c_chain, base + 2)
                    dve.tensor_tensor(mrest[:, :], mc[:, :], m3[:, 0, :], ALU.subtract).then_inc(c_chain, 1)
                if products_in(s, u):
                    quarter = (u - 1) % 4
                    for pair in range(2):
                        k = 8 * s - 10 + 2 * u + pair
                        eb = 4 * quarter + 2 * pair
                        dve.wait_ge(xa_ready, k + 1)
                        dve.scalar_tensor_tensor(xacc[:, eb:eb + 2, :],
                                                 ps[:, (XACC + pair) * BANK:(XACC + pair + 1) * BANK].rearrange("p (e d) -> p e d", e=2),
                                                 1.0 / (D_SCALE * XLN_SCALE), xacc[:, eb:eb + 2, :],
                                                 ALU.mult, ALU.add).then_inc(xa_read, 1)
                if logits_in(s) and u % 2 == 1:
                    dve.wait_ge(c_chain, base + 4)
                    dve.tensor_tensor(m3[:, 2, :], mrest[:, :], m3[:, 1, :], ALU.subtract).then_inc(c_chain, 1)
                if turns(s, u):
                    keep_turned(2 * s + u // 2 - 1)
            supers(dve, run)


def experts(nc, m, ps, tag, xacc, yt, ew, eb_in):
    RING = 4
    with phase_of(nc, tag) as (ctx, sem, sb):
        w = sb("w", [P, RING, 4, DC, D])
        bias = sb("bias", [P, EB, D])
        xT = sb("xT", [P, DC, SLOTS])
        stats, mv = sb("stats", [P, EB, 6]), sb("mv", [P, EB, 2])
        ve, sdv, rs = sb("ve", [P, EB]), sb("sdv", [P, EB]), sb("rs", [P, EB])
        w_loaded = [sem(f"w_loaded{i}") for i in range(RING)]
        b_loaded = sem("b_loaded")
        clipped, stats_done, mv_done, ve_done = sem("clipped"), sem("stats_done"), sem("mv_done"), sem("ve_done")
        sd_done, rs_done, normed, tanh_done = sem("sd_done"), sem("rs_done"), sem("normed"), sem("tanh_done")
        filled, copied = sem("filled"), sem("copied")
        y_ready, y_kept = sem("y_ready"), sem("y_kept")
        block = ctx.enter_context(nc.Block())

        @block.sync
        def _(sp):
            for b in range(EB):
                if b == 1:
                    for j in range(4):
                        sp.dma_start(bias[32 * j:32 * j + 32, :, :],
                                     eb_in.rearrange("(b j) d -> j b d", j=4)[j, :, :].partition_broadcast(32)).then_inc(b_loaded, 16)
                wait(sp, y_ready, b - RING + 1)
                for j in range(4):
                    sp.dma_start(w[:, b % RING, j, :, :], ew[4 * b + j].rearrange("(c p) h -> p c h", p=P)).then_inc(w_loaded[b % RING], 16)

        @block.vector
        def _(dve):
            dve.tensor_scalar(xacc[:, :, :], xacc[:, :, :], -33000.0, 65000.0, ALU.max, ALU.min).then_inc(clipped, 1)
            dve.wait_ge(clipped, 1)
            for b in range(EB):
                dve.bn_stats(stats[:, b, :], xacc[:, b, :]).then_inc(stats_done, 1)
            for b in range(EB):
                dve.wait_ge(stats_done, b + 1)
                dve.bn_aggr(mv[:, b, :], stats[:, b, :]).then_inc(mv_done, 1)
            dve.wait_ge(mv_done, EB)
            dve.tensor_scalar(ve[:, :], mv[:, :, 1], EPS, None, ALU.add).then_inc(ve_done, 1)
            dve.wait_ge(sd_done, 1)
            dve.reciprocal(rs[:, :], sdv[:, :]).then_inc(rs_done, 1)
            dve.wait_ge(rs_done, 1)
            for b in range(EB):
                dve.tensor_scalar(xacc[:, b, :], xacc[:, b, :], mv[:, b, 0:1], rs[:, b:b + 1],
                                  ALU.subtract, ALU.mult).then_inc(normed, 1)
            for i in range(EB // 4 * DC):
                bg, c = divmod(i, DC)
                dve.wait_ge(filled, i + 1)
                dve.tensor_copy(xT[:, c, bg * BANK:(bg + 1) * BANK], ps[:, (i % 4) * BANK:(i % 4 + 1) * BANK]).then_inc(copied, 1)
            dve.wait_ge(b_loaded, 64)
            for b in range(EB):
                dve.wait_ge(y_ready, b + 1)
                dve.tensor_tensor(yt[:, b, :], ps[:, (4 + b % 4) * BANK:(4 + b % 4) * BANK + D], bias[:, b, :],
                                  ALU.add).then_inc(y_kept, 1)

        @block.scalar
        def _(act):
            act.wait_ge(ve_done, 1)
            act.activation(sdv[:, :], ve[:, :], ACT.Sqrt).then_inc(sd_done, 1)
            for b in range(0, EB, 4):
                act.wait_ge(normed, b + 4)
                act.activation(xacc[:, b:b + 4, :], xacc[:, b:b + 4, :], ACT.Tanh).then_inc(tanh_done, 1)

        @block.tensor
        def _(pe):
            for i in range(EB // 4 * DC):
                bg, c = divmod(i, DC)
                pe.wait_ge(tanh_done, bg + 1)
                wait(pe, copied, i - 3)
                for k in range(4):
                    mm = pe.transpose(ps[:, (i % 4) * BANK + k * P:(i % 4) * BANK + (k + 1) * P],
                                      xacc[:, 4 * bg + k, c * P:(c + 1) * P], m.ident[:, :])
                mm.then_inc(filled, 1)
            pe.wait_ge(copied, EB // 4 * DC)
            for b in range(EB):
                pe.wait_ge(w_loaded[b % RING], 64 * (b // RING + 1))
                wait(pe, y_kept, b - 3)
                for c in range(DC):
                    for j in range(4):
                        n0 = (4 * b + j) * PS
                        mm = pe.matmul(ps[32 * j:32 * j + 32, (4 + b % 4) * BANK:(4 + b % 4) * BANK + D],
                                       xT[:, c, n0:n0 + PS], w[:, b % RING, j, c, :], start=(c == 0), stop=(c == DC - 1))
                mm.then_inc(y_ready, 1)


def combine(nc, m, ps, tag, xlnT, phi, pbcol, mct, yt, out):
    AHEAD = 10
    TURNS = [("exp", b) for b in range(AHEAD - 4)]
    for i in range(4):
        TURNS += [("high", i), ("exp", AHEAD - 4 + i)]
    for b in range(AHEAD, EB):
        TURNS += [("exp", b), ("high", 4 + 2 * (b - AHEAD)), ("high", 5 + 2 * (b - AHEAD))]
    NT = 3
    with phase_of(nc, tag) as (ctx, sem, sb):
        ct = [sb(f"ct{i}", [P, EB, BANK]) for i in range(2)]
        ctp = [t[:, :, :].bitcast(F16) for t in ct]
        norm = sb("norm", [P, NT, BANK])
        csum = sb("csum", [P, BANK])
        rsum = sb("rsum", [P, BANK])
        yp = sb("yp", [P, 2, EB, D], F16)
        LT, Y = 0, 4
        SUM = GATHER = 7

        lt_ready = sem("lt_ready")
        ct_exp = sem("ct_exp")
        added = sem("added")
        sum_ready = sem("sum_ready")
        r_ready = sem("r_ready")
        normed = sem("normed")
        high = sem("high")
        c_ready = sem("c_ready")
        y_ready = sem("y_ready")
        x_added = sem("x_added")
        y_chain = sem("y_chain")
        gathered = sem("gathered")
        y_cut = sem("y_cut")
        stored = sem("stored")
        scales = Scales(sb, "y")
        block = ctx.enter_context(nc.Block())

        def groups(eng, run):
            run(0, 0, True, False)
            with eng.Fori(0, G // 2 - 1) as it:
                run(2 * it + 1, 1, True, True)
                run(2 * it + 2, 0, True, True)
            run(G - 1, 1, True, True)
            run(G, 0, False, True)

        @block.tensor
        def _(pe):
            def run(g, parity, logits, products):
                def logits_t(b):
                    n = EB * g + b
                    wait(pe, ct_exp, n - 3)
                    o = ps[:, (LT + b % 4) * BANK:(LT + b % 4 + 1) * BANK]
                    for i, (xp, pp, c) in enumerate(TERMS):
                        pe.matmul(o, phi[:, pp, c, b * P:(b + 1) * P],
                                  xlnT[:, xp:xp + 1, c, bass.ds(g * BANK, BANK)].rearrange("p a n -> p (a n)"),
                                  start=(i == 0), stop=False)
                    pe.matmul(o, m.sameneg[0:3 * PS, :], mct[0:3 * PS, bass.ds(g * BANK, BANK)],
                              start=False, stop=True).then_inc(lt_ready, 1)

                def product(i):
                    quarter, zt = divmod(i, 4)
                    if zt == 0:
                        pe.wait_ge(c_ready, EB * (g - 1) + 4 * quarter + 4)
                    for kb in range(4 * quarter, 4 * quarter + 4):
                        for k, (cp, y) in enumerate(((0, 0), (0, 1), (1, 0))):
                            mm = pe.matmul(ps[:, (Y + zt) * BANK:(Y + zt) * BANK + D],
                                           ctp[1 - parity][:, kb, cp * BANK + zt * P:cp * BANK + (zt + 1) * P], yp[:, y, kb, :],
                                           start=(kb == 0 and k == 0), stop=(kb == EB - 1 and k == 2))
                    if i == EB - 1:
                        mm.then_inc(y_ready, 1)

                def total():
                    pe.wait_ge(y_cut, 2)
                    pe.wait_ge(x_added, g)
                    pe.wait_ge(added, (EB - 1) * g)
                    pe.matmul(ps[:, SUM * BANK:(SUM + 1) * BANK], m.same[:, :], csum[:, :],
                              start=True, stop=True).then_inc(sum_ready, 1)

                if logits:
                    for b in range(AHEAD):
                        logits_t(b)
                        if b == 1 and products:
                            total()
                else:
                    total()
                if not products:
                    scales.gather(pe, m, ps[:, GATHER * BANK:GATHER * BANK + P], y_chain, gathered)
                for i in range(EB):
                    if products:
                        product(i)
                    if logits and i + AHEAD < EB:
                        logits_t(i + AHEAD)
            groups(pe, run)

        @block.scalar
        def _(act):
            def run(g, parity, logits, products):
                if logits:
                    wait(act, y_ready, g)
                for what, b in TURNS:
                    if what == "exp" and logits:
                        act.wait_ge(lt_ready, EB * g + b + 1)
                        act.activation(ct[parity][:, b, :], ps[:, (LT + b % 4) * BANK:(LT + b % 4 + 1) * BANK], ACT.Exp,
                                       bias=pbcol[:, b:b + 1], scale=m.unscale[:, 0:1]).then_inc(ct_exp, 1)
                    if what == "high" and products:
                        act.wait_ge(normed, EB * (g - 1) + b + 1)
                        act.copy(ctp[1 - parity][:, b, 0:BANK], norm[:, b % NT, :]).then_inc(high, 1)
            groups(act, run)

        @block.gpsimd
        def _(pool):
            pool.sem_inc(y_ready, 1)
            pool.sem_inc(x_added, 1)

            def run(g, parity, logits, products):
                if not logits:
                    return
                wait(pool, sum_ready, g)
                for b in range(1, EB):
                    n = (EB - 1) * g + b - 1
                    pool.wait_ge(ct_exp, EB * g + b + 1)
                    wait(pool, added, n)
                    pool.tensor_tensor(csum[:, :], ct[parity][:, 0, :] if b == 1 else csum[:, :],
                                       ct[parity][:, b, :], ALU.add).then_inc(added, 1)
            groups(pool, run)

        @block.vector
        def _(dve):
            y_f = yt[:, :, :].rearrange("p e d -> p (e d)")
            yp_f = yp[:, :, :, :].rearrange("p i e d -> p i (e d)")
            n_y = scales.make(dve, y_f, ps[:, GATHER * BANK:GATHER * BANK + P], y_chain, gathered)
            dve.tensor_scalar(scales.scale[:, :], scales.inverse[:, :], TOP, None, ALU.mult).then_inc(y_chain, 1)
            dve.tensor_scalar(scales.back[:, :], scales.power[:, :], 1.0 / (TOP * D_SCALE), None, ALU.mult).then_inc(y_chain, 1)
            dve.wait_ge(y_chain, n_y + 2)
            scales.cut(dve, y_f, yp_f, y_cut)

            def run(g, parity, logits, products):
                if not products:
                    return
                dve.wait_ge(sum_ready, g)
                dve.reciprocal(rsum[:, :], ps[:, SUM * BANK:(SUM + 1) * BANK]).then_inc(r_ready, 1)
                dve.wait_ge(r_ready, 2 * g - 1)
                dve.tensor_scalar(rsum[:, :], rsum[:, :], D_SCALE, None, ALU.mult).then_inc(r_ready, 1)
                dve.wait_ge(r_ready, 2 * g)
                c, parts = ct[1 - parity], ctp[1 - parity]

                def low(b):
                    dve.wait_ge(high, EB * (g - 1) + b + 1)
                    dve.tensor_tensor(parts[:, b, BANK:2 * BANK], norm[:, b % NT, :], parts[:, b, 0:BANK],
                                      ALU.subtract).then_inc(c_ready, 1)

                dve.wait_ge(x_added, g)
                for b in range(EB):
                    if b >= NT:
                        dve.wait_ge(c_ready, EB * (g - 1) + b - NT + 1)
                    dve.tensor_tensor(norm[:, b % NT, :], c[:, b, :], rsum[:, :], ALU.mult).then_inc(normed, 1)
                    if b > 0:
                        low(b - 1)
                low(EB - 1)
                dve.wait_ge(y_ready, g + 1)
                for half in range(2):
                    xt = m.x[:, bass.ds(4 * (g - 1) + 2 * half, 2), :]
                    banks = ps[:, (Y + 2 * half) * BANK:(Y + 2 * half + 2) * BANK].rearrange("p (a n) -> p a n", a=2)
                    last = dve.scalar_tensor_tensor(xt, banks[:, :, 0:D],
                                                    scales.back[:, 0:1], xt, ALU.mult, ALU.add)
                last.then_inc(x_added, 1)
            groups(dve, run)

        @block.sync
        def _(sp):
            if out is None:
                return
            o = out.rearrange("a (t p) d -> p (a t) d", p=P)

            def run(g, parity, logits, products):
                if products:
                    sp.wait_ge(x_added, g + 1)
                    sp.dma_start(o[:, bass.ds(4 * (g - 1), 4), :], m.x[:, bass.ds(4 * (g - 1), 4), :]).then_inc(stored, 16)
            groups(sp, run)
            sp.wait_ge(stored, 16 * G)


def build(nc, t, out):
    with ExitStack() as ctx:
        sb = lambda n, shape, dt=F32: ctx.enter_context(nc.sbuf_tensor(n, shape, dt))
        ps_t = ctx.enter_context(nc.psum_tensor("ps", [P, 8 * BANK], F32))
        ps = ps_t[:, :]
        m = Kept()
        m.x = sb("x", [P, T, D])
        m.ident, m.identb = sb("ident", [P, P]), sb("identb", [P, P], BF16)
        m.mask_qk = sb("mask_qk", [P, P], BF16)
        m.sel, m.same, m.sameneg = sb("sel", [P, HD + 1]), sb("same", [P, P]), sb("sameneg", [P, P], BF16)
        m.onesb = sb("onesb", [P, P], BF16)
        m.unscale = sb("unscale", [P, 1])
        phi_parts = nc.dram_tensor("phi_parts", (2, P, DC, SLOTS), F16).ap()
        pb_parts = nc.dram_tensor("pb_parts", (1, 3, SLOTS), BF16).ap()
        load_and_cut(nc, m, ps, t["x"], t["phi_wT"], t["phi_b"], phi_parts, pb_parts)

        def attention_layer(tag, wq, wk, wv, wo, bias, denom_bias):
            parts_q = nc.dram_tensor(f"{tag}_parts_q", (3, D, N), BF16).ap()
            parts_k = nc.dram_tensor(f"{tag}_parts_k", (3, D, N), BF16).ap()
            with nc.sbuf_tensor(f"{tag}_attn", [P, T, D], F32) as attn:
                with nc.sbuf_tensor(f"{tag}_v", [P, T, D], F32) as v:
                    with nc.sbuf_tensor(f"{tag}_xlnT", [P, DC, N], F32) as xlnT:
                        layernorm(nc, m, ps, f"{tag}_ln", attn, xlnT)
                        project_qkv(nc, m, ps, f"{tag}_qkv", xlnT, v, wq, wk, wv, parts_q, parts_k)
                    attention(nc, m, ps, f"{tag}_att", v, attn, parts_q, parts_k, denom_bias)
                project_out(nc, m, ps, f"{tag}_out", attn, wo, bias)

        def mixture_layer(tag, last):
            with ExitStack() as c2:
                sb2 = lambda n, shape, dt=F32: c2.enter_context(nc.sbuf_tensor(f"{tag}_{n}", shape, dt))
                xlnT, xacc = sb2("xlnT", [P, 2, DC, N], F16), sb2("xacc", [P, EB, D])
                phi, pb3 = sb2("phi", [P, 2, DC, SLOTS], F16), sb2("pb3", [3, SLOTS], BF16)
                mct, pbcol = sb2("mct", [3 * PS, N], BF16), sb2("pbcol", [P, EB])
                loads = [(phi[:, part, :, :], phi_parts[part]) for part in range(2)]
                loads += [(pb3[0:3, :], pb_parts.rearrange("a i s -> (a i) s")), (pbcol[:, :], t["phi_bT"])]
                with nc.sbuf_tensor(f"{tag}_xtok", [P, T, 2, D], F16) as xtok:
                    with nc.sbuf_tensor(f"{tag}_xln", [P, T, D], F32) as xln:
                        layernorm(nc, m, ps, f"{tag}_ln", xln, xlnT, xtok, loads)
                    dispatch(nc, m, ps, f"{tag}_disp", xtok, xlnT, phi, pb3, xacc, mct)
                experts(nc, m, ps, f"{tag}_exp", xacc, xacc, t["expert_w"], t["expert_b"])
                combine(nc, m, ps, f"{tag}_comb", xlnT, phi, pbcol, mct, xacc, out if last else None)

        attention_layer("a", t["a_WqT"], t["a_WkT"], t["a_WvT"], t["a_WoT"], t["a_bo"], t["a_db"])
        mixture_layer("f", False)
        attention_layer("b", t["b_WqT"], t["b_WkT"], t["b_WvT"], t["b_WoT"], None, None)
        mixture_layer("g", True)


def kernel(**inputs):
    import numpy as _np
    import concourse.bacc as _bacc
    from concourse import mybir as _mybir
    from concourse.bass_utils import run_bass_kernel_spmd as _run

    arrays = {"x": inputs["L0_attn_a_x"]}
    for short, name in (("q", "Wq"), ("k", "Wk"), ("v", "Wv"), ("o", "Wo")):
        arrays[f"a_W{short}T"] = _np.asarray(inputs[f"L0_attn_a_{name}"]).T
        arrays[f"b_W{short}T"] = _np.asarray(inputs[f"L0_attn_b_{short}_proj_weight"]).T
    arrays["a_bo"] = inputs["L0_attn_a_bo"]
    arrays["a_db"] = inputs["L0_attn_a_denom_bias"]
    arrays["phi_wT"] = _np.asarray(inputs["L0_ffn_phi_w"]).T
    arrays["phi_b"] = inputs["L0_ffn_phi_b"]
    arrays["phi_bT"] = _np.asarray(inputs["L0_ffn_phi_b"]).reshape(EB, P).T
    arrays["expert_w"] = inputs["L0_ffn_expert_w"]
    arrays["expert_b"] = inputs["L0_ffn_expert_b"]

    nc = _bacc.Bacc("TRN2", target_bir_lowering=False, num_devices=1)
    given, t = {}, {}
    for name, a in arrays.items():
        a = _np.ascontiguousarray(a)
        given[f"in_{name}"] = a
        t[name] = nc.dram_tensor(f"in_{name}", a.shape, _mybir.dt.from_np(a.dtype), kind="ExternalInput").ap()
    out = nc.dram_tensor("out", (1, N, D), _mybir.dt.float32, kind="ExternalOutput").ap()
    build(nc, t, out)
    r = _run(nc, [given], core_ids=[0])
    return r.results[0]["out"]
```
